# Optimizing a Trainium2 kernel written in Bass

```python
import numpy as np
import jax
import jax.numpy as jnp

def _softmax(x, axis=-1):
    return jax.nn.softmax(x, axis=axis)

def _gelu(x):
    return jax.nn.gelu(x, approximate=True)

def _silu(x):
    return jax.nn.silu(x)

def _sigmoid(x):
    return jax.nn.sigmoid(x)

def _layernorm(x, axis=-1, eps=1e-05):
    m = jnp.mean(x, axis=axis, keepdims=True)
    v = jnp.var(x, axis=axis, keepdims=True)
    return (x - m) / jnp.sqrt(v + eps)

def _scatter_add(tgt, idx, src, axis=0):
    return tgt.at[idx].add(src)

def _segment_sum(src, seg, n):
    return jax.ops.segment_sum(src, seg, n)
kernel_name = 'mk_adaln_ffn_d1_seqx_r4_4272a4'

def setup_inputs(seed: int=0):
    np.random.seed(seed)
    _w = jnp.asarray

    def _rec_inputs():
        import jax
        import jax.numpy as jnp
        _rk = jax.random.key(seed)
        x = -0.000125 + 0.9999 * jax.random.normal(jax.random.fold_in(_rk, 1), (128, 64, 1024), jnp.float32)
        _lenS = 64 - jax.random.randint(jax.random.fold_in(_rk, 7), (128,), 0, max(1, 64 // 4) + 1, jnp.int32)
        _lenS2 = 64 - jax.random.randint(jax.random.fold_in(_rk, 8), (128,), 0, max(1, 64 // 4) + 1, jnp.int32)
        cond_128 = 0.0061147 + 1.02565 * jax.random.normal(jax.random.fold_in(_rk, 11), (128, 128), jnp.float32)
        return (x, cond_128)
    x, cond_128 = _rec_inputs()

    def _L0_cond_setup():
        import jax, jax.numpy as jnp
        import numpy as np
        K = 8
        T = 1.0
        D_EMBD = 128
        IN_C = 64
        OUT_C = 64
        BS = 32
        H = 1024
        HID = 128
        key = jax.random.key(seed)
        ks = jax.random.split(key, 10)
        s = lambda fan_in: 1.0 / np.sqrt(fan_in)
        return {'x': jax.random.normal(ks[0], (BS, IN_C, H), dtype=jnp.float32), 'embedding': jax.random.normal(ks[1], (BS, D_EMBD), dtype=jnp.float32), 'W0': jax.random.normal(ks[2], (D_EMBD, HID), dtype=jnp.float32) * s(D_EMBD), 'b0': jnp.zeros((HID,), dtype=jnp.float32), 'W1': jax.random.normal(ks[3], (HID, HID), dtype=jnp.float32) * s(HID), 'b1': jnp.zeros((HID,), dtype=jnp.float32), 'W2': jax.random.normal(ks[4], (HID, K), dtype=jnp.float32) * s(HID), 'b2': jnp.zeros((K,), dtype=jnp.float32), 'weight': jax.random.normal(ks[5], (K, OUT_C, IN_C, 1), dtype=jnp.float32) * s(IN_C), 'bias_k': jax.random.normal(ks[6], (K, OUT_C), dtype=jnp.float32) * 0.1}
    _L0_cond_all = _L0_cond_setup()
    _L0_cond_in = {k: v for k, v in _L0_cond_all.items() if k in ('W0', 'b0', 'W1', 'b1', 'W2', 'b2', 'weight', 'bias_k')}
    del _L0_cond_all

    def _L0_ffn_setup():
        import jax, jax.numpy as jnp
        import numpy as np
        K_TOP = 8
        key = jax.random.key(seed)
        k1, k2, k3 = jax.random.split(key, 3)
        B, S, H, E = (4, 1024, 1024, 64)
        hidden_states = jax.random.normal(k1, (B, S, H), dtype=jnp.float32)
        router_weight = jax.random.normal(k2, (E, H), dtype=jnp.float32)
        router_bias = jnp.zeros((E,), dtype=jnp.float32)
        expert_bias = jax.random.normal(k3, (E, H), dtype=jnp.float32) * 0.1
        return {'hidden_states': hidden_states, 'router_weight': router_weight, 'router_bias': router_bias, 'expert_bias': expert_bias}
    _L0_ffn_all = _L0_ffn_setup()
    _L0_ffn_in = {k: v for k, v in _L0_ffn_all.items() if k in ('router_weight', 'router_bias', 'expert_bias')}
    del _L0_ffn_all
    return {'x': x, 'cond_128': cond_128, 'L0_cond_W0': _L0_cond_in['W0'], 'L0_cond_b0': _L0_cond_in['b0'], 'L0_cond_W1': _L0_cond_in['W1'], 'L0_cond_b1': _L0_cond_in['b1'], 'L0_cond_W2': _L0_cond_in['W2'], 'L0_cond_b2': _L0_cond_in['b2'], 'L0_cond_weight': _L0_cond_in['weight'], 'L0_cond_bias_k': _L0_cond_in['bias_k'], 'L0_ffn_router_weight': _L0_ffn_in['router_weight'], 'L0_ffn_router_bias': _L0_ffn_in['router_bias'], 'L0_ffn_expert_bias': _L0_ffn_in['expert_bias']}

def reference(x, cond_128, L0_cond_W0, L0_cond_b0, L0_cond_W1, L0_cond_b1, L0_cond_W2, L0_cond_b2, L0_cond_weight, L0_cond_bias_k, L0_ffn_router_weight, L0_ffn_router_bias, L0_ffn_expert_bias):
    import jax
    import jax.numpy as jnp

    def _L0_cond_ref(x, embedding, W0, b0, W1, b1, W2, b2, weight, bias_k):
        import jax, jax.numpy as jnp
        import numpy as np
        K = 8
        T = 1.0
        D_EMBD = 128
        IN_C = 64
        OUT_C = 64
        BS = 32
        H = 1024
        HID = 128
        h = jax.nn.gelu(embedding @ W0 + b0, approximate=False)
        h = jax.nn.gelu(h @ W1 + b1, approximate=False)
        att = jax.nn.softmax((h @ W2 + b2) / T, axis=-1)
        agg_w = jnp.einsum('bk,koi->boi', att, weight[..., 0])
        agg_b = att @ bias_k
        out = jnp.einsum('boi,bih->boh', agg_w, x) + agg_b[:, :, None]
        return out

    def _L0_ffn_ref(hidden_states, router_weight, router_bias, expert_bias):
        import jax, jax.numpy as jnp
        import numpy as np
        K_TOP = 8
        B, S, H = hidden_states.shape
        E = router_weight.shape[0]
        T = B * S
        flat = hidden_states.reshape(T, H)
        logits = jnp.einsum('th,eh->te', flat, router_weight) + router_bias
        scores = jax.nn.softmax(logits, axis=-1)
        topk_w, topk_idx = jax.lax.top_k(scores, K_TOP)
        w_sum = topk_w.sum(axis=-1, keepdims=True)
        w_dense = jnp.zeros((T, E), dtype=scores.dtype).at[jnp.arange(T)[:, None], topk_idx].add(topk_w)
        bias_mix = jnp.einsum('te,eh->th', w_dense, expert_bias)
        out = flat * w_sum + bias_mix
        return out.reshape(B, S, H)
    x = x + _L0_ffn_ref(_L0_cond_ref(x, cond_128, L0_cond_W0, L0_cond_b0, L0_cond_W1, L0_cond_b1, L0_cond_W2, L0_cond_b2, L0_cond_weight, L0_cond_bias_k), L0_ffn_router_weight, L0_ffn_router_bias, L0_ffn_expert_bias)
    return x

_drawn_inputs = setup_inputs


def setup_inputs(seed=0):
    import zlib

    import numpy as np

    out = dict(_drawn_inputs(seed))
    spreads = {'L0_cond_b0': (0.0, 0.524),
     'L0_cond_b1': (0.0, 0.291),
     'L0_cond_b2': (0.0, 0.278),
     'L0_ffn_router_bias': (0.0, 2.0)}
    factors = {}
    for name, (base, spread) in spreads.items():
        noise = np.random.default_rng([zlib.crc32(name.encode()), seed]).standard_normal(out[name].shape)
        drawn = base * np.exp(spread * noise) if base else spread * noise
        out[name] = jnp.asarray(drawn.astype(out[name].dtype))
    for name, factor in factors.items():
        out[name] = (out[name] * factor).astype(out[name].dtype)
    return out
```

```python
import concourse.bass as bass
from concourse import mybir
from contextlib import ExitStack
import itertools

FP32 = mybir.dt.float32
ALU = mybir.AluOpType
ACT = mybir.ActivationFunctionType
AX = mybir.AxisListType

P = 128
B, C, H = 128, 64, 1024
K = 8
NE = 64
TOP = 8
D = 128
PAIR = P // C
NJ = B // PAIR
GT = 4
NG = NJ // GT
TILE = P * H
HC = H // P
BANK = 512
HH = H // BANK
UNITS = GT * HH
CU = BANK // P
OS = 8
GS = C // OS
SLOTS = 2 * GT
STEADY = 4
DVE_UNITS = (3, 7)
ACT_UNITS = tuple(u for u in range(UNITS) if u not in DVE_UNITS)
STEPS = 10


def adaln_ffn_kernel(nc, x, cond, w0, b0, w1, b1, w2, b2, weight, bias_k, router, router_bias, expert_bias, out):
    x_tiles = x.rearrange("b c h -> (b c) h").rearrange("(j p) h -> j p h", p=P)
    x_flat, out_flat = x.rearrange("b c h -> (b c h)"), out.rearrange("b c h -> (b c h)")
    w_koi = weight.rearrange("k o i u -> k o (i u)")

    def tile_at(flat, start):
        return flat[bass.ds(start, TILE)].rearrange("(p h) -> p h", p=P)

    ctx = ExitStack()
    with ctx:
        def sb(name, shape):
            return ctx.enter_context(nc.sbuf_tensor(name, shape, FP32))

        def bank(name):
            return ctx.enter_context(nc.psum_tensor(name, [P, BANK], FP32))

        def sem(name):
            return ctx.enter_context(nc.semaphore(name))

        x_sb = sb("x_sb", [P, SLOTS, H])
        xe_sb = sb("xe_sb", [P, GT, PAIR, H])
        xT_sb = sb("xT_sb", [P, HC, GT * P])
        out_sb = sb("out_sb", [P, GT, H])
        zT_sb = sb("zT_sb", [P, GT * P])
        z_sb = sb("z_sb", [P, GT, P])
        at_blocks = sb("at_blocks", [P, GT, P])
        logit_bias = sb("logit_bias", [P, GT, NE])
        logit_part = sb("logit_part", [P, GT, NE])
        logits = sb("logits", [P, GT, NE])
        shifted = sb("shifted", [P, GT, NE])
        expd = sb("expd", [P, GT, NE])
        rest = sb("rest", [P, GT, NE])
        kept = sb("kept", [P, GT, NE])
        row_max = sb("row_max", [P, GT])
        top8 = sb("top8", [P, GT, TOP])
        exp_sum = sb("exp_sum", [P, GT])
        top_sum = sb("top_sum", [P, GT])
        inv_sum = sb("inv_sum", [P, GT])
        w_sum = sb("w_sum", [P, GT])
        out_bias = sb("out_bias", [P, 2, GT])
        mix = sb("mix", [P, GT, C + NE])
        mixT_sb = sb("mixT_sb", [P, GT, P])
        a_all = sb("a_all", [P, NJ, C])
        aT_all = sb("aT_all", [P, NJ, C])
        ab_all = sb("ab_all", [P, NJ])
        rT_sb = sb("rT_sb", [P, HC, NE])
        r_sum = sb("r_sum", [P, NE])
        rb_sb = sb("rb_sb", [P, NE])
        ident = sb("ident", [P, P])
        eye2 = sb("eye2", [P, C])
        ones = sb("ones", [P, P])
        own_half = sb("own_half", [P, PAIR])
        own_slice = sb("own_slice", [P, OS])
        cond_sb = sb("cond_sb", [B, D])
        condT_sb = sb("condT_sb", [D, B])
        w0_sb, w1_sb, w2_sb = sb("w0_sb", [D, D]), sb("w1_sb", [D, D]), sb("w2_sb", [D, K])
        b0_sb, b1_sb, b2_sb = sb("b0_sb", [D, 1]), sb("b1_sb", [D, 1]), sb("b2_sb", [B, K])
        h1T_sb, h2T_sb = sb("h1T_sb", [D, B]), sb("h2T_sb", [D, B])
        att_logits, att_shifted, att_exp = sb("att_logits", [B, K]), sb("att_shifted", [B, K]), sb("att_exp", [B, K])
        att_max, att_total, att_inv = sb("att_max", [B, 1]), sb("att_total", [B, 1]), sb("att_inv", [B, 1])
        att_wide = sb("att_wide", [B, PAIR, K, OS])
        att_diag = sb("att_diag", [P, OS, NJ])
        router_sb = sb("router_sb", [NE, H])
        w_rows = sb("w_rows", [P, GS, PAIR, C])
        w_o = sb("w_o", [C, PAIR, K, C])
        w_cols = sb("w_cols", [P, GS, PAIR, C])
        bias_rows = sb("bias_rows", [P, PAIR, C])

        xT_ps = [bank("xT_ps0"), bank("xT_ps1")]
        out_ps = [bank("out_ps0"), bank("out_ps1")]
        zT_ps, z_ps, logit_ps, mixT_ps = bank("zT_ps"), bank("z_ps"), bank("logit_ps"), bank("mixT_ps")
        condT_ps, h1_ps, h2_ps, att_ps = mixT_ps[:, 0:B], mixT_ps[:, B:2 * B], mixT_ps[:, 2 * B:3 * B], mixT_ps[:, 3 * B:3 * B + K]
        rT_ps = z_ps[:, 0:HC * NE]
        r_sum_ps, w_cols_ps = out_ps[0][:, 0:NE], out_ps[1][:, 0:GS * C]
        attT_ps, ab_ps = logit_ps[:, 0:B], logit_ps[:, B:B + NJ]

        net_loaded = sem("net_loaded")
        mats_loaded = sem("mats_loaded")
        router_loaded = sem("router_loaded")
        experts_loaded = sem("experts_loaded")
        x_loaded = [sem(f"x_loaded{s}") for s in range(SLOTS)]
        stored = [sem(f"stored{k}") for k in range(GT)]
        consts_set = sem("consts_set")
        zeros_set = sem("zeros_set")
        net_pe = sem("net_pe")
        net_act = sem("net_act")
        net_dve = sem("net_dve")
        rT_done, rT_kept = sem("rT_done"), sem("rT_kept")
        r_sum_done, r_sum_kept = sem("r_sum_done"), sem("r_sum_kept")
        w_cols_done, w_cols_kept = sem("w_cols_done"), sem("w_cols_kept")
        dve_consts = sem("dve_consts")
        ab_done, ab_kept = sem("ab_done"), sem("ab_kept")
        a_done = sem("a_done")
        a_kept_act, a_kept_dve = sem("a_kept_act"), sem("a_kept_dve")
        xT_done, xT_kept = sem("xT_done"), sem("xT_kept")
        zT_done, zT_kept = sem("zT_done"), sem("zT_kept")
        z_done, z_kept = sem("z_done"), sem("z_kept")
        logits_done = sem("logits_done")
        blocks_ready, logit_bias_ready = sem("blocks_ready"), sem("logit_bias_ready")
        shifted_ready, exp_ready = sem("shifted_ready"), sem("exp_ready")
        w_sum_ready, mix_a_ready, mix_w_ready = sem("w_sum_ready"), sem("mix_a_ready"), sem("mix_w_ready")
        mixT_done, mixT_kept = sem("mixT_done"), sem("mixT_kept")
        chain = sem("chain")
        pool_bias, pool_mix = sem("pool_bias"), sem("pool_mix")
        xe_ready = sem("xe_ready")
        out_done = sem("out_done")
        out_kept_act, out_kept_dve = sem("out_kept_act"), sem("out_kept_dve")

        def out_kept(group, unit):
            if unit in DVE_UNITS:
                return out_kept_dve, len(DVE_UNITS) * group + DVE_UNITS.index(unit) + 1
            return out_kept_act, len(ACT_UNITS) * group + ACT_UNITS.index(unit) + 1

        def iterations(eng, body, first=1, last=NG):
            for g in range(first, STEADY):
                body(g, g % 2)
            with eng.Fori(0, (last - STEADY) // 2) as n:
                for parity in range(2):
                    body(2 * n + (STEADY + parity), parity, n)
            for g in range(last, NG + 2):
                body(g, g % 2)

        def loads(g, parity, n, older=0):
            return (g - older) // 2 + 1 if n is None else n + STEADY // 2 + 1 - (older if parity == 0 else 0)

        def stages(g, n):
            return (True, True, True) if n is not None else (g < NG, 1 <= g <= NG, 2 <= g)

        block = ctx.enter_context(nc.Block())

        @block.sync
        def _(sp):
            sp.dma_start(router_sb[:], router).then_inc(router_loaded, 16)
            sp.dma_start(rb_sb[:], router_bias.partition_broadcast(P)).then_inc(router_loaded, 16)
            for s in range(SLOTS):
                sp.dma_start(x_sb[:, s, :], x_tiles[s]).then_inc(x_loaded[s], 16)
                if s == GT - 1:
                    for k in range(GT):
                        for p in range(PAIR):
                            sp.dma_start(xe_sb[C:P, k, p, :], expert_bias).then_inc(experts_loaded, 16)

            def early(value):
                register = sp.alloc_register(f"early{next(names)}")
                sp.reg_mov(register, value)
                return sp.snap(register, min_val=0, max_val=UNITS * NG)

            names = itertools.count()

            def body(g, parity, n=None):
                transposing, _, putting_out = stages(g, n)
                load_at = [GT * TILE * (g + 1) + TILE * k for k in range(GT)]
                store_at = [GT * TILE * (g - 2) + TILE * k for k in range(GT)]
                slot_free = [GT * (g - 1) + k + 1 for k in range(GT)]
                kept = [out_kept(g - 2, u) for u in range(UNITS)]
                if n is not None:
                    kept = [(s, early(v)) for s, v in kept]
                for k in range(GT):
                    if n is not None or (transposing and 1 <= g <= NG - 2):
                        s = (1 - parity) * GT + k
                        sp.wait_ge(xe_ready, slot_free[k])
                        sp.dma_start(x_sb[:, s, :], tile_at(x_flat, load_at[k])).then_inc(x_loaded[s], 16)
                    if putting_out:
                        for h in range(HH):
                            sp.wait_ge(*kept[HH * k + h])
                        sp.dma_start(tile_at(out_flat, store_at[k]), out_sb[:, k, :]).then_inc(stored[k], 16)

            iterations(sp, body, last=NG - 2)
            for k in range(GT):
                sp.wait_ge(stored[k], 16 * NG)

        @block.gpsimd
        def _(pool):
            pool.memset(ident[:], 0.0).then_inc(consts_set, 1)
            pool.wait_ge(consts_set, 1)
            pool.affine_select(out=ident[:], in_=ident[:], compare_op=ALU.not_equal, fill=1.0, base=0,
                               pattern=[[-1, P]], channel_multiplier=1).then_inc(consts_set, 1)
            pool.memset(ones[:], 1.0).then_inc(consts_set, 1)
            pool.wait_ge(r_sum_kept, 1)
            pool.wait_ge(router_loaded, 32)
            pool.wait_ge(ab_kept, 1)
            pool.wait_ge(a_kept_act, GS)
            pool.wait_ge(a_kept_dve, GS)
            pool.wait_ge(dve_consts, 3)

            def body(g, parity, n=None):
                _, routing, _ = stages(g, n)
                if not routing:
                    return
                q = g - 1
                if n is not None or q >= 1:
                    pool.wait_ge(logits_done, q)
                pool.tensor_tensor(at_blocks[:].rearrange("p k (a c) -> p k a c", a=PAIR),
                                   aT_all[:, bass.ds(GT * q, GT), :].unsqueeze(2).to_broadcast([P, GT, PAIR, C]),
                                   own_half[:].unsqueeze(1).unsqueeze(3).to_broadcast([P, GT, PAIR, C]),
                                   ALU.mult).then_inc(blocks_ready, 1)
                if n is not None or q >= 1:
                    pool.wait_ge(shifted_ready, q)
                pool.tensor_tensor(logit_bias[:], ab_all[:, bass.ds(GT * q, GT)].unsqueeze(2).to_broadcast([P, GT, NE]),
                                   r_sum[:].unsqueeze(1).to_broadcast([P, GT, NE]), ALU.mult).then_inc(pool_bias, 1)
                pool.wait_ge(pool_bias, q + 1)
                pool.tensor_tensor(logit_bias[:], logit_bias[:], rb_sb[:].unsqueeze(1).to_broadcast([P, GT, NE]),
                                   ALU.add).then_inc(logit_bias_ready, 1)
                if n is not None or q >= 1:
                    pool.wait_ge(mixT_done, q)
                pool.wait_ge(w_sum_ready, q + 1)
                pool.tensor_tensor(mix[:, :, 0:C], a_all[:, bass.ds(GT * q, GT), :],
                                   w_sum[:].unsqueeze(2).to_broadcast([P, GT, C]), ALU.mult).then_inc(pool_mix, 1)
                pool.wait_ge(pool_mix, q + 1)
                pool.tensor_tensor(mix[:, :, 0:C], mix[:, :, 0:C], eye2[:].unsqueeze(1).to_broadcast([P, GT, C]),
                                   ALU.add).then_inc(mix_a_ready, 1)

            iterations(pool, body)

        @block.scalar
        def _(act):
            act.dma_start(cond_sb[:], cond).then_inc(net_loaded, 16)
            act.dma_start(w0_sb[:], w0).then_inc(net_loaded, 16)
            act.dma_start(b0_sb[:], b0.unsqueeze(1)).then_inc(net_loaded, 16)
            act.dma_start(w1_sb[:], w1).then_inc(net_loaded, 16)
            act.dma_start(b1_sb[:], b1.unsqueeze(1)).then_inc(net_loaded, 16)
            act.dma_start(w2_sb[:], w2).then_inc(net_loaded, 16)
            act.dma_start(b2_sb[:], b2.partition_broadcast(B)).then_inc(net_loaded, 16)
            for p in range(PAIR):
                act.dma_start(w_o[:, p, :, :], w_koi.rearrange("k o i -> o k i")).then_inc(mats_loaded, 16)
            for p in range(PAIR):
                rows = slice(C * p, C * p + C)
                if p == 0:
                    act.wait_ge(zeros_set, 1)
                act.dma_start(w_rows[rows, :, p, :], w_koi.rearrange("k (s g) i -> (k s) g i", g=GS)).then_inc(mats_loaded, 16)
                act.dma_start(bias_rows[rows, p, :],
                              bias_k.unsqueeze(1).to_broadcast([K, OS, C])).then_inc(mats_loaded, 16)

            def keep_xT(g, u):
                act.wait_ge(xT_done, UNITS * g + u + 1)
                k, h = u // HH, u % HH
                nc.scalar.activation(xT_sb[:, CU * h:CU * h + CU, P * k:P * k + P],
                                     xT_ps[h][:].rearrange("p (c t) -> p c t", c=CU), ACT.Copy).then_inc(xT_kept, 1)

            def keep_out(g, parity, u, n):
                q, k, h = g - 2, u // HH, u % HH
                if n is not None or q >= 1:
                    act.wait_ge(stored[k], 16 * q)
                act.wait_ge(out_done, UNITS * q + u + 1)
                nc.scalar.activation(out_sb[:, k, BANK * h:BANK * h + BANK], out_ps[h][:], ACT.Identity,
                                     bias=out_bias[:, parity, k:k + 1]).then_inc(out_kept_act, 1)

            def body(g, parity, n=None):
                transposing, routing, putting_out = stages(g, n)
                if routing:
                    act.wait_ge(zT_done, g)
                    nc.scalar.activation(zT_sb[:], zT_ps[:], ACT.Copy).then_inc(zT_kept, 1)
                for u in range(UNITS):
                    if transposing and u >= 1:
                        keep_xT(g, u)
                    if transposing and u == 0:
                        keep_xT(g, 0)
                    if routing and u == 2:
                        act.wait_ge(z_done, g)
                        nc.scalar.activation(z_sb[:], z_ps[:].rearrange("p (k n) -> p k n", k=GT), ACT.Copy).then_inc(z_kept, 1)
                    if routing and u == 5:
                        act.wait_ge(shifted_ready, g)
                        nc.scalar.activation(expd[:], shifted[:], ACT.Exp).then_inc(exp_ready, 1)
                    if putting_out and u >= 1 and u - 1 in ACT_UNITS:
                        keep_out(g, parity, u - 1, n)
                if putting_out and UNITS - 1 in ACT_UNITS:
                    keep_out(g, parity, UNITS - 1, n)

            act.wait_ge(net_pe, 1)
            nc.scalar.activation(condT_sb[:], condT_ps, ACT.Copy).then_inc(net_act, 1)
            act.wait_ge(net_loaded, 16 * 7)
            act.wait_ge(net_pe, 2)
            nc.scalar.activation(h1T_sb[:], h1_ps, ACT.Gelu, bias=b0_sb[:, 0:1]).then_inc(net_act, 1)
            for u in range(0, 4):
                keep_xT(0, u)
            act.wait_ge(net_pe, 3)
            nc.scalar.activation(h2T_sb[:], h2_ps, ACT.Gelu, bias=b1_sb[:, 0:1]).then_inc(net_act, 1)
            for u in range(4, UNITS):
                keep_xT(0, u)
            act.wait_ge(net_dve, 3)
            nc.scalar.activation(att_exp[:], att_shifted[:], ACT.Exp).then_inc(net_act, 1)
            for s in range(GS):
                act.wait_ge(a_done, 2 * s + 1)
                nc.scalar.activation(aT_all[:].rearrange("p j (a s) -> p a j s", s=GS)[:, :, :, s],
                                     out_ps[0][:].rearrange("p (a j) -> p a j", a=OS), ACT.Copy).then_inc(a_kept_act, 1)
            iterations(act, body)

        @block.vector
        def _(dve):
            for p in range(PAIR):
                rows = slice(C * p, C * p + C)
                nc.vector.memset(w_rows[rows, :, 1 - p, :], 0.0)
                nc.vector.memset(bias_rows[rows, 1 - p, :], 0.0)
                last = nc.vector.memset(w_cols[rows, :, 1 - p, :], 0.0)
            last.then_inc(zeros_set, 1)
            dve.wait_ge(zeros_set, 1)
            dve.wait_ge(consts_set, 2)
            nc.vector.tensor_tensor(eye2[:], ident[:, 0:C], ident[:, C:P], ALU.add).then_inc(dve_consts, 1)
            nc.vector.tensor_reduce(own_slice[:], ident[:].rearrange("p (q s) -> p s q", s=OS), AX.X, ALU.add).then_inc(dve_consts, 1)
            nc.vector.tensor_reduce(own_half[:], ident[:].rearrange("p (a c) -> p a c", a=PAIR), AX.X, ALU.add).then_inc(dve_consts, 1)
            dve.wait_ge(rT_done, 1)
            nc.vector.tensor_copy(rT_sb[:], rT_ps.rearrange("p (c e) -> p c e", c=HC)).then_inc(rT_kept, 1)
            dve.wait_ge(r_sum_done, 1)
            nc.vector.tensor_copy(r_sum[:], r_sum_ps).then_inc(r_sum_kept, 1)
            dve.wait_ge(w_cols_done, 1)
            for p in range(PAIR):
                rows = slice(C * p, C * p + C)
                last = nc.vector.tensor_copy(w_cols[rows, :, p, :], w_cols_ps[rows].rearrange("p (s o) -> p s o", s=GS))
            last.then_inc(w_cols_kept, 1)
            dve.wait_ge(net_loaded, 16 * 7)
            dve.wait_ge(net_pe, 4)
            nc.vector.tensor_tensor(att_logits[:], att_ps, b2_sb[:], ALU.add).then_inc(net_dve, 1)
            dve.wait_ge(net_dve, 1)
            nc.vector.tensor_reduce(att_max[:], att_logits[:], AX.X, ALU.max).then_inc(net_dve, 1)
            dve.wait_ge(net_dve, 2)
            nc.vector.tensor_scalar(att_shifted[:], att_logits[:], att_max[:, 0:1], None, ALU.subtract).then_inc(net_dve, 1)
            dve.wait_ge(net_act, 4)
            nc.vector.tensor_reduce(att_total[:], att_exp[:], AX.X, ALU.add).then_inc(net_dve, 1)
            dve.wait_ge(net_dve, 4)
            nc.vector.reciprocal(att_inv[:], att_total[:]).then_inc(net_dve, 1)
            dve.wait_ge(net_dve, 5)
            nc.vector.tensor_scalar(att_wide[:].rearrange("b p k s -> b p (k s)").rearrange("b p (k s) -> b p k s", k=K),
                                    att_exp[:].unsqueeze(1).unsqueeze(3).to_broadcast([B, PAIR, K, OS]),
                                    att_inv[:, 0:1], None, ALU.mult).then_inc(net_dve, 1)
            dve.wait_ge(dve_consts, 2)
            dve.wait_ge(net_pe, 5)
            for p in range(PAIR):
                rows = slice(C * p, C * p + C)
                mine = attT_ps[rows].rearrange("r (j p) -> r p j", p=PAIR)[:, p, :]
                nc.vector.tensor_tensor(att_diag[rows], mine.unsqueeze(1).to_broadcast([C, OS, NJ]),
                                        own_slice[rows].unsqueeze(2).to_broadcast([C, OS, NJ]), ALU.mult).then_inc(net_dve, 1)
            dve.wait_ge(ab_done, 1)
            nc.vector.tensor_copy(ab_all[:], ab_ps).then_inc(ab_kept, 1)
            for s in range(GS):
                dve.wait_ge(a_done, 2 * s + 2)
                nc.vector.tensor_copy(a_all[:].rearrange("p j (a s) -> p a j s", s=GS)[:, :, :, s],
                                      out_ps[1][:].rearrange("p (a j) -> p a j", a=OS)).then_inc(a_kept_dve, 1)

            def body(g, parity, n=None):
                _, routing, putting_out = stages(g, n)
                q = g - 1

                def step(n):
                    dve.wait_ge(chain, STEPS * q + n)

                def copy_x(k):
                    s = (1 - parity) * GT + k
                    dve.wait_ge(x_loaded[s], 16 * loads(g, parity, n, older=1))
                    if n is not None or g >= 2:
                        dve.wait_ge(out_done, UNITS * (g - 2) + HH * (k + 1))
                    for p in range(PAIR):
                        last = nc.vector.tensor_copy(xe_sb[0:C, k, p, :], x_sb[C * p:C * p + C, s, :])
                    last.then_inc(xe_ready, 1)

                def keep_out(u):
                    k, h = u // HH, u % HH
                    if n is not None or g >= 3:
                        dve.wait_ge(stored[k], 16 * (g - 2))
                    dve.wait_ge(out_done, UNITS * (g - 2) + u + 1)
                    nc.vector.tensor_scalar(out_sb[:, k, BANK * h:BANK * h + BANK], out_ps[h][:],
                                            out_bias[:, parity, k:k + 1], None, ALU.add).then_inc(out_kept_dve, 1)

                if routing:
                    copy_x(0)
                    halves = logit_ps[:].rearrange("p (k s e) -> p k s e", k=GT, s=2)
                    dve.wait_ge(logit_bias_ready, q + 1)
                    dve.wait_ge(logits_done, q + 1)
                    nc.vector.tensor_tensor(logit_part[:], halves[:, :, 0, :], logit_bias[:], ALU.add).then_inc(chain, 1)
                    step(1)
                    nc.vector.tensor_tensor(logits[:], halves[:, :, 1, :], logit_part[:], ALU.add).then_inc(chain, 1)
                    step(2)
                    nc.vector.tensor_reduce(row_max[:], logits[:], AX.X, ALU.max).then_inc(chain, 1)
                    step(3)
                    nc.vector.tensor_tensor(shifted[:], logits[:], row_max[:].unsqueeze(2).to_broadcast([P, GT, NE]),
                                            ALU.subtract).then_inc(shifted_ready, 1)
                    copy_x(1)
                if putting_out and 3 in DVE_UNITS:
                    keep_out(3)
                if routing:
                    dve.wait_ge(exp_ready, q + 1)
                    nc.vector.tensor_reduce(exp_sum[:], expd[:], AX.X, ALU.add).then_inc(chain, 1)
                    for k in range(GT):
                        last = nc.vector.max(top8[:, k, :], expd[:, k, :])
                    last.then_inc(chain, 1)
                    step(4)
                    nc.vector.reciprocal(inv_sum[:], exp_sum[:]).then_inc(chain, 1)
                    step(5)
                    nc.vector.tensor_reduce(top_sum[:], top8[:], AX.X, ALU.add).then_inc(chain, 1)
                    for k in range(GT):
                        last = nc.vector.match_replace(rest[:, k, :], top8[:, k, :], expd[:, k, :], 0.0)
                    last.then_inc(chain, 1)
                    step(7)
                    nc.vector.tensor_tensor(w_sum[:], top_sum[:], inv_sum[:], ALU.mult).then_inc(w_sum_ready, 1)
                    step(8)
                    nc.vector.tensor_tensor(kept[:], expd[:], rest[:], ALU.subtract).then_inc(chain, 1)
                    dve.wait_ge(w_sum_ready, q + 1)
                    nc.vector.tensor_tensor(out_bias[:, 1 - parity, :], w_sum[:], ab_all[:, bass.ds(GT * q, GT)],
                                            ALU.mult).then_inc(chain, 1)
                    if n is not None or q >= 1:
                        dve.wait_ge(mixT_done, q)
                    step(9)
                    nc.vector.tensor_tensor(mix[:, :, C:C + NE], kept[:], inv_sum[:].unsqueeze(2).to_broadcast([P, GT, NE]),
                                            ALU.mult).then_inc(mix_w_ready, 1)
                    copy_x(2)
                    copy_x(3)
                if putting_out and 7 in DVE_UNITS:
                    keep_out(7)
                if routing:
                    dve.wait_ge(mixT_done, q + 1)
                    nc.vector.tensor_copy(mixT_sb[:], mixT_ps[:].rearrange("p (k t) -> p k t", k=GT)).then_inc(mixT_kept, 1)

            iterations(dve, body)

        @block.tensor
        def _(pe):
            def transpose_x(g, parity, u, x_loads, n=None):
                k, h = u // HH, u % HH
                if h == 0:
                    pe.wait_ge(x_loaded[parity * GT + k], 16 * x_loads)
                if n is not None or UNITS * g + u >= HH:
                    pe.wait_ge(xT_kept, UNITS * g + u - HH + 1)
                for c in range(CU):
                    last = nc.tensor.transpose(xT_ps[h][:, P * c:P * c + P],
                                               x_sb[:, parity * GT + k, P * (CU * h + c):P * (CU * h + c + 1)], ident[:])
                last.then_inc(xT_done, 1)

            def make_zT(g):
                pe.wait_ge(xT_kept, UNITS * g + UNITS)
                for c in range(HC):
                    half = C * (c % 2)
                    last = nc.tensor.matmul(zT_ps[half:half + NE, :], rT_sb[:, c, :], xT_sb[:, c, :],
                                            start=(c < 2), stop=(c >= HC - 2))
                last.then_inc(zT_done, 1)

            def make_z(g):
                pe.wait_ge(zT_kept, g)
                for k in range(GT):
                    last = nc.tensor.transpose(z_ps[:, P * k:P * k + P], zT_sb[:, P * k:P * k + P], ident[:])
                last.then_inc(z_done, 1)

            def make_logits(g):
                pe.wait_ge(blocks_ready, g)
                pe.wait_ge(z_kept, g)
                for k in range(GT):
                    last = nc.tensor.matmul(logit_ps[:, P * k:P * k + P], at_blocks[:, k, :], z_sb[:, k, :], start=True, stop=True)
                last.then_inc(logits_done, 1)

            def make_mixT(g):
                pe.wait_ge(mix_a_ready, g)
                pe.wait_ge(mix_w_ready, g)
                for k in range(GT):
                    last = nc.tensor.transpose(mixT_ps[:, P * k:P * k + P], mix[:, k, :], ident[:])
                last.then_inc(mixT_done, 1)

            def make_out(g, u, n):
                q, k, h = g - 2, u // HH, u % HH
                if u == 0:
                    pe.wait_ge(mixT_kept, q + 1)
                if h == 0:
                    pe.wait_ge(xe_ready, GT * q + k + 1)
                if u >= HH:
                    pe.wait_ge(*out_kept(q, u - HH))
                elif n is not None or q >= 1:
                    pe.wait_ge(*out_kept(q - 1, UNITS + u - HH))
                for p in range(PAIR):
                    last = nc.tensor.matmul(out_ps[h][C * p:C * p + C, :], mixT_sb[:, k, C * p:C * p + C],
                                            xe_sb[:, k, p, BANK * h:BANK * h + BANK], start=True, stop=True)
                last.then_inc(out_done, 1)

            def body(g, parity, n=None):
                transposing, routing, putting_out = stages(g, n)
                x_loads = loads(g, parity, n)
                for u in range(UNITS + 1):
                    if transposing and u < UNITS:
                        transpose_x(g, parity, u, x_loads, n)
                    if routing and u == 2:
                        make_z(g)
                    if putting_out and u >= 1:
                        make_out(g, u - 1, n)
                    if routing and u == 3:
                        make_logits(g)
                if transposing:
                    make_zT(g)
                if routing:
                    make_mixT(g)

            pe.wait_ge(consts_set, 2)
            pe.wait_ge(net_loaded, 16 * 7)
            nc.tensor.transpose(condT_ps, cond_sb[:], ident[:]).then_inc(net_pe, 1)
            pe.wait_ge(router_loaded, 32)
            for c in range(HC):
                last = nc.tensor.transpose(rT_ps[:, NE * c:NE * c + NE], router_sb[:, P * c:P * c + P], ident[0:NE, 0:NE])
            last.then_inc(rT_done, 1)
            pe.wait_ge(net_act, 1)
            nc.tensor.matmul(h1_ps, w0_sb[:], condT_sb[:], start=True, stop=True).then_inc(net_pe, 1)
            pe.wait_ge(mats_loaded, 16 * 6)
            for s in range(GS):
                last = nc.tensor.transpose(w_cols_ps[:, C * s:C * s + C],
                                           w_o[:].rearrange("o p k (a s) -> o (p k a) s", s=GS)[:, :, s], ident[0:C, 0:C])
            last.then_inc(w_cols_done, 1)
            for u in range(0, 2):
                transpose_x(0, 0, u, 1)
            pe.wait_ge(consts_set, 3)
            pe.wait_ge(rT_kept, 1)
            for c in range(HC):
                last = nc.tensor.matmul(r_sum_ps, ones[:], rT_sb[:, c, :], start=(c == 0), stop=(c == HC - 1))
            last.then_inc(r_sum_done, 1)
            pe.wait_ge(net_act, 2)
            nc.tensor.matmul(h2_ps, w1_sb[:], h1T_sb[:], start=True, stop=True).then_inc(net_pe, 1)
            for u in range(2, 5):
                transpose_x(0, 0, u, 1)
            pe.wait_ge(net_act, 3)
            nc.tensor.matmul(att_ps, h2T_sb[:], w2_sb[:], start=True, stop=True).then_inc(net_pe, 1)
            for u in range(5, UNITS):
                transpose_x(0, 0, u, 1)
            make_zT(0)
            pe.wait_ge(net_dve, 6)
            nc.tensor.transpose(attT_ps, att_wide[:].rearrange("b p k s -> b (p k s)"), ident[:]).then_inc(net_pe, 1)
            pe.wait_ge(net_dve, 8)
            pe.wait_ge(zeros_set, 1)
            nc.tensor.matmul(ab_ps, bias_rows[:].rearrange("p a o -> p (a o)"), att_diag[:, 0, :], start=True, stop=True).then_inc(ab_done, 1)
            pe.wait_ge(w_cols_kept, 1)
            pe.wait_ge(r_sum_kept, 1)
            for s in range(GS):
                if s:
                    pe.wait_ge(a_kept_act, s)
                nc.tensor.matmul(out_ps[0][:], w_rows[:, s, :, :].rearrange("p a i -> p (a i)"),
                                 att_diag[:].rearrange("p a j -> p (a j)"), start=True, stop=True).then_inc(a_done, 1)
                if s:
                    pe.wait_ge(a_kept_dve, s)
                nc.tensor.matmul(out_ps[1][:], w_cols[:, s, :, :].rearrange("p a o -> p (a o)"),
                                 att_diag[:].rearrange("p a j -> p (a j)"), start=True, stop=True).then_inc(a_done, 1)
            pe.wait_ge(a_kept_act, GS)
            pe.wait_ge(a_kept_dve, GS)
            pe.wait_ge(experts_loaded, 16 * GT * PAIR)

            iterations(pe, body)


_INS = ['x', 'cond_128', 'L0_cond_W0', 'L0_cond_b0', 'L0_cond_W1', 'L0_cond_b1', 'L0_cond_W2', 'L0_cond_b2',
        'L0_cond_weight', 'L0_cond_bias_k', 'L0_ffn_router_weight', 'L0_ffn_router_bias', 'L0_ffn_expert_bias']
_OUTS = [((B, C, H), 'float32')]


def kernel(**inputs):
    import numpy as _np
    import concourse.bacc as _bacc
    from concourse import mybir as _mybir
    from concourse.bass_utils import run_bass_kernel_spmd as _run

    nc = _bacc.Bacc("TRN2", target_bir_lowering=False, num_devices=1)
    arrays, args = {}, []
    for name in _INS:
        a = _np.ascontiguousarray(inputs[name])
        arrays[f"in_{name}_dram"] = a
        args.append(nc.dram_tensor(f"in_{name}_dram", a.shape, _mybir.dt.from_np(a.dtype), kind="ExternalInput").ap())
    for i, (shape, dtype) in enumerate(_OUTS):
        dt = _mybir.dt.from_np(_np.dtype(dtype))
        args.append(nc.dram_tensor(f"out_{i}_dram", shape, dt, kind="ExternalOutput").ap())
    adaln_ffn_kernel(nc, *args)
    r = _run(nc, [arrays], core_ids=[0])
    got = tuple(r.results[0][f"out_{i}_dram"] for i in range(len(_OUTS)))
    return got[0]
```

```python
import concourse.bass as bass
from concourse import mybir
from contextlib import ExitStack
import itertools

FP32 = mybir.dt.float32
ALU = mybir.AluOpType
ACT = mybir.ActivationFunctionType
AX = mybir.AxisListType

P = 128
B, C, H = 128, 64, 1024
K = 8
NE = 64
TOP = 8
D = 128
PAIR = P // C
NJ = B // PAIR
GT = 4
NG = NJ // GT
TILE = P * H
HC = H // P
BANK = 512
HH = H // BANK
UNITS = GT * HH
CU = BANK // P
OS = 8
GS = C // OS
SLOTS = 2 * GT
STEADY = 4
STEPS = 9


def adaln_ffn_kernel(nc, x, cond, w0, b0, w1, b1, w2, b2, weight, bias_k, router, router_bias, expert_bias, out):
    x_tiles = x.rearrange("b c h -> (b c) h").rearrange("(j p) h -> j p h", p=P)
    x_flat, out_flat = x.rearrange("b c h -> (b c h)"), out.rearrange("b c h -> (b c h)")
    w_koi = weight.rearrange("k o i u -> k o (i u)")

    def tile_at(flat, start):
        return flat[bass.ds(start, TILE)].rearrange("(p h) -> p h", p=P)

    ctx = ExitStack()
    with ctx:
        def sb(name, shape):
            return ctx.enter_context(nc.sbuf_tensor(name, shape, FP32))

        def bank(name):
            return ctx.enter_context(nc.psum_tensor(name, [P, BANK], FP32))

        def sem(name):
            return ctx.enter_context(nc.semaphore(name))

        x_sb = sb("x_sb", [P, SLOTS, H])
        xe_sb = sb("xe_sb", [P, GT, PAIR, H])
        xT_sb = sb("xT_sb", [P, HC, GT * P])
        out_sb = sb("out_sb", [P, GT, H])
        zT_sb = sb("zT_sb", [P, PAIR * P])
        z_sb = sb("z_sb", [P, GT + 1, NE])
        at_blocks = sb("at_blocks", [P, GT, P])
        logit_bias = sb("logit_bias", [P, GT, NE])
        logits = sb("logits", [P, GT, NE])
        shifted = sb("shifted", [P, GT, NE])
        expd = sb("expd", [P, GT, NE])
        rest = sb("rest", [P, GT, NE])
        kept = sb("kept", [P, GT, NE])
        row_max = sb("row_max", [P, GT])
        top8 = sb("top8", [P, GT, TOP])
        exp_sum = sb("exp_sum", [P, GT])
        top_sum = sb("top_sum", [P, GT])
        inv_sum = sb("inv_sum", [P, GT])
        w_sum = sb("w_sum", [P, GT])
        out_bias = sb("out_bias", [P, 2, GT])
        mix = sb("mix", [P, GT, C + NE])
        mixT_sb = sb("mixT_sb", [P, GT, P])
        aT_all = sb("aT_all", [P, NJ, C])
        aT_top = sb("aT_top", [C, NJ, PAIR, C])
        ab_all = sb("ab_all", [P, NJ])
        rT_sb = sb("rT_sb", [P, HC, NE])
        r_sum = sb("r_sum", [P, NE])
        rb_sb = sb("rb_sb", [P, NE])
        ident = sb("ident", [P, P])
        ones = sb("ones", [P, P])
        own_half = sb("own_half", [P, PAIR])
        own_slice = sb("own_slice", [P, OS])
        cond_sb = sb("cond_sb", [B, D])
        condT_sb = sb("condT_sb", [D, B])
        w0_sb, w1_sb, w2_sb = sb("w0_sb", [D, D]), sb("w1_sb", [D, D]), sb("w2_sb", [D, K])
        b0_sb, b1_sb, b2_sb = sb("b0_sb", [D, 1]), sb("b1_sb", [D, 1]), sb("b2_sb", [B, K])
        h1T_sb, h2T_sb = sb("h1T_sb", [D, B]), sb("h2T_sb", [D, B])
        att_logits, att_shifted, att_exp = sb("att_logits", [B, K]), sb("att_shifted", [B, K]), sb("att_exp", [B, K])
        att_max, att_total, att_inv = sb("att_max", [B, 1]), sb("att_total", [B, 1]), sb("att_inv", [B, 1])
        att_wide = sb("att_wide", [B, PAIR, K, OS])
        att_diag = sb("att_diag", [P, OS, NJ])
        router_sb = sb("router_sb", [NE, H])
        w_rows = sb("w_rows", [P, GS, PAIR, C])
        bias_rows = sb("bias_rows", [P, PAIR, C])

        xT_ps = [bank("xT_ps0"), bank("xT_ps1")]
        out_ps = [bank("out_ps0"), bank("out_ps1")]
        zT_ps, z_ps, logit_ps, mixT_ps = bank("zT_ps"), bank("z_ps"), bank("logit_ps"), bank("mixT_ps")
        condT_ps, h1_ps, h2_ps, att_ps = mixT_ps[:, 0:B], mixT_ps[:, B:2 * B], mixT_ps[:, 2 * B:3 * B], mixT_ps[:, 3 * B:3 * B + K]
        rT_ps, r_sum_ps = z_ps[:, 0:HC * NE], out_ps[0][:, 0:NE]
        attT_ps, ab_ps = logit_ps[:, 0:B], logit_ps[:, B:B + NJ]

        net_loaded = [sem(f"net_loaded{layer}") for layer in range(3)]
        mats_loaded = sem("mats_loaded")
        router_loaded = sem("router_loaded")
        experts_loaded = sem("experts_loaded")
        x_loaded = [sem(f"x_loaded{s}") for s in range(SLOTS)]
        stored = [sem(f"stored{k}") for k in range(GT)]
        consts_set = sem("consts_set")
        zeros_set = sem("zeros_set")
        net_pe = sem("net_pe")
        net_act = sem("net_act")
        net_dve = sem("net_dve")
        rT_done, rT_kept = sem("rT_done"), sem("rT_kept")
        r_sum_done, r_sum_kept = sem("r_sum_done"), sem("r_sum_kept")
        dve_consts = sem("dve_consts")
        ab_done, ab_kept = sem("ab_done"), sem("ab_kept")
        aT_done = sem("aT_done")
        aT_kept_act, aT_kept_dve = sem("aT_kept_act"), sem("aT_kept_dve")
        aT_top_ready = sem("aT_top_ready")
        xT_done, xT_kept = sem("xT_done"), sem("xT_kept")
        zT_done, zT_kept = sem("zT_done"), sem("zT_kept")
        z_done, z_kept = sem("z_done"), sem("z_kept")
        logits_done = sem("logits_done")
        blocks_ready, logit_bias_ready = sem("blocks_ready"), sem("logit_bias_ready")
        shifted_ready, exp_ready = sem("shifted_ready"), sem("exp_ready")
        mix_ready, mixT_done, mixT_scaled = sem("mix_ready"), sem("mixT_done"), sem("mixT_scaled")
        out_bias_ready = sem("out_bias_ready")
        mixT_x_ready, mixT_e_ready = sem("mixT_x_ready"), sem("mixT_e_ready")
        chain = sem("chain")
        logit_bias_scaled = sem("logit_bias_scaled")
        xe_ready = sem("xe_ready")
        out_done = sem("out_done")
        out_kept = sem("out_kept")

        def iterations(eng, body, first=1, last=NG):
            for g in range(first, STEADY):
                body(g, g % 2)
            with eng.Fori(0, (last - STEADY) // 2) as n:
                for parity in range(2):
                    body(2 * n + (STEADY + parity), parity, n)
            for g in range(last, NG + 2):
                body(g, g % 2)

        def loads(g, parity, n, older=0):
            return (g - older) // 2 + 1 if n is None else n + STEADY // 2 + 1 - (older if parity == 0 else 0)

        def stages(g, n):
            return (True, True, True) if n is not None else (g < NG, 1 <= g <= NG, 2 <= g)

        def aT_slice(s):
            return aT_all[:].rearrange("p j (a s) -> p a j s", s=GS)[:, :, :, s]

        block = ctx.enter_context(nc.Block())

        @block.sync
        def _(sp):
            def load_x(s):
                sp.dma_start(x_sb[:, s, :], x_tiles[s]).then_inc(x_loaded[s], 16)

            load_x(0)
            sp.dma_start(router_sb[:], router).then_inc(router_loaded, 16)
            sp.dma_start(rb_sb[:], router_bias.partition_broadcast(P)).then_inc(router_loaded, 16)
            for s in range(1, SLOTS):
                load_x(s)
            for k in range(GT):
                for p in range(PAIR):
                    sp.dma_start(xe_sb[C:P, k, p, :], expert_bias).then_inc(experts_loaded, 16)

            def early(value):
                register = sp.alloc_register(f"early{next(names)}")
                sp.reg_mov(register, value)
                return sp.snap(register, min_val=0, max_val=UNITS * NG)

            names = itertools.count()

            def body(g, parity, n=None):
                transposing, _, putting_out = stages(g, n)
                load_at = [GT * TILE * (g + 1) + TILE * k for k in range(GT)]
                store_at = [GT * TILE * (g - 2) + TILE * k for k in range(GT)]
                slot_free = [GT * (g - 1) + k + 1 for k in range(GT)]
                kept = [UNITS * (g - 2) + HH * (k + 1) for k in range(GT)]
                if n is not None:
                    kept = [early(v) for v in kept]
                for k in range(GT):
                    if n is not None or (transposing and 1 <= g <= NG - 2):
                        s = (1 - parity) * GT + k
                        sp.wait_ge(xe_ready, slot_free[k])
                        sp.dma_start(x_sb[:, s, :], tile_at(x_flat, load_at[k])).then_inc(x_loaded[s], 16)
                    if putting_out:
                        sp.wait_ge(out_kept, kept[k])
                        sp.dma_start(tile_at(out_flat, store_at[k]), out_sb[:, k, :]).then_inc(stored[k], 16)

            iterations(sp, body, last=NG - 2)
            for k in range(GT):
                sp.wait_ge(stored[k], 16 * NG)

        @block.gpsimd
        def _(pool):
            pool.memset(ident[:], 0.0).then_inc(consts_set, 1)
            pool.wait_ge(consts_set, 1)
            pool.affine_select(out=ident[:], in_=ident[:], compare_op=ALU.not_equal, fill=1.0, base=0,
                               pattern=[[-1, P]], channel_multiplier=1).then_inc(consts_set, 1)
            pool.memset(ones[:], 1.0).then_inc(consts_set, 1)
            pool.wait_ge(r_sum_kept, 1)
            pool.wait_ge(router_loaded, 32)
            pool.wait_ge(ab_kept, 1)
            pool.wait_ge(aT_kept_act, GS // 2)
            pool.wait_ge(aT_kept_dve, GS // 2)
            pool.wait_ge(dve_consts, 2)

            def body(g, parity, n=None):
                _, routing, _ = stages(g, n)
                if not routing:
                    return
                q = g - 1
                if n is not None or q >= 1:
                    pool.wait_ge(logits_done, q)
                pool.tensor_tensor(at_blocks[:].rearrange("p k (a c) -> p k a c", a=PAIR),
                                   aT_all[:, bass.ds(GT * q, GT), :].unsqueeze(2).to_broadcast([P, GT, PAIR, C]),
                                   own_half[:].unsqueeze(1).unsqueeze(3).to_broadcast([P, GT, PAIR, C]),
                                   ALU.mult).then_inc(blocks_ready, 1)
                if n is not None or q >= 1:
                    pool.wait_ge(shifted_ready, q)
                pool.tensor_tensor(logit_bias[:], ab_all[:, bass.ds(GT * q, GT)].unsqueeze(2).to_broadcast([P, GT, NE]),
                                   r_sum[:].unsqueeze(1).to_broadcast([P, GT, NE]), ALU.mult).then_inc(logit_bias_scaled, 1)
                pool.wait_ge(logit_bias_scaled, q + 1)
                pool.tensor_tensor(logit_bias[:], logit_bias[:], rb_sb[:].unsqueeze(1).to_broadcast([P, GT, NE]),
                                   ALU.add).then_inc(logit_bias_ready, 1)

            iterations(pool, body)

        @block.scalar
        def _(act):
            act.dma_start(cond_sb[:], cond).then_inc(net_loaded[0], 16)
            act.dma_start(w0_sb[:], w0).then_inc(net_loaded[0], 16)
            act.dma_start(b0_sb[:], b0.unsqueeze(1)).then_inc(net_loaded[0], 16)
            act.dma_start(w1_sb[:], w1).then_inc(net_loaded[1], 16)
            act.dma_start(b1_sb[:], b1.unsqueeze(1)).then_inc(net_loaded[1], 16)
            act.dma_start(w2_sb[:], w2).then_inc(net_loaded[2], 16)
            act.dma_start(b2_sb[:], b2.partition_broadcast(B)).then_inc(net_loaded[2], 16)
            act.wait_ge(zeros_set, 1)
            for p in range(PAIR):
                rows = slice(C * p, C * p + C)
                act.dma_start(w_rows[rows, :, p, :], w_koi.rearrange("k (s g) i -> (k s) g i", g=GS)).then_inc(mats_loaded, 16)
                act.dma_start(bias_rows[rows, p, :],
                              bias_k.unsqueeze(1).to_broadcast([K, OS, C])).then_inc(mats_loaded, 16)

            def keep_xT(g, u):
                act.wait_ge(xT_done, UNITS * g + u + 1)
                k, h = u // HH, u % HH
                nc.scalar.activation(xT_sb[:, CU * h:CU * h + CU, P * k:P * k + P],
                                     xT_ps[h][:].rearrange("p (c t) -> p c t", c=CU), ACT.Copy).then_inc(xT_kept, 1)

            def keep_out(g, parity, u, n):
                q, k, h = g - 2, u // HH, u % HH
                if h == 0 and (n is not None or q >= 1):
                    act.wait_ge(stored[k], 16 * q)
                if u == 0:
                    act.wait_ge(out_bias_ready, q + 1)
                act.wait_ge(out_done, UNITS * q + u + 1)
                nc.scalar.activation(out_sb[:, k, BANK * h:BANK * h + BANK], out_ps[h][:], ACT.Identity,
                                     bias=out_bias[:, parity, k:k + 1]).then_inc(out_kept, 1)

            def keep_z(g):
                act.wait_ge(z_done, g)
                nc.scalar.activation(z_sb[:, 0:GT, :], z_ps[:, 0:GT * NE].rearrange("p (m e) -> p m e", m=GT),
                                     ACT.Copy).then_inc(z_kept, 1)

            def body(g, parity, n=None):
                transposing, routing, putting_out = stages(g, n)
                if routing:
                    act.wait_ge(zT_done, g)
                    nc.scalar.activation(zT_sb[:], zT_ps[:, 0:PAIR * P], ACT.Copy).then_inc(zT_kept, 1)
                    if not transposing:
                        keep_z(g)
                for u in range(UNITS + 1):
                    if transposing and u < UNITS:
                        keep_xT(g, u)
                    if routing and transposing and u == 1:
                        keep_z(g)
                    if putting_out and u >= 1:
                        keep_out(g, parity, u - 1, n)
                    if routing and u == 3:
                        act.wait_ge(shifted_ready, g)
                        nc.scalar.activation(expd[:], shifted[:], ACT.Exp).then_inc(exp_ready, 1)
                if routing:
                    act.wait_ge(mixT_done, g)
                    nc.scalar.activation(mixT_sb[C:P], mixT_ps[C:P, :].rearrange("p (k t) -> p k t", k=GT),
                                         ACT.Copy).then_inc(mixT_e_ready, 1)

            act.wait_ge(net_pe, 1)
            nc.scalar.activation(condT_sb[:], condT_ps, ACT.Copy).then_inc(net_act, 1)
            act.wait_ge(net_loaded[0], 48)
            act.wait_ge(net_pe, 2)
            nc.scalar.activation(h1T_sb[:], h1_ps, ACT.Gelu, bias=b0_sb[:, 0:1]).then_inc(net_act, 1)
            act.wait_ge(net_loaded[1], 32)
            act.wait_ge(net_pe, 3)
            nc.scalar.activation(h2T_sb[:], h2_ps, ACT.Gelu, bias=b1_sb[:, 0:1]).then_inc(net_act, 1)
            for u in range(0, 2):
                keep_xT(0, u)
            act.wait_ge(net_dve, 3)
            nc.scalar.activation(att_exp[:], att_shifted[:], ACT.Exp).then_inc(net_act, 1)
            for u in range(2, UNITS):
                keep_xT(0, u)
            for s in range(0, GS, 2):
                act.wait_ge(aT_done, s + 1)
                nc.scalar.activation(aT_slice(s), out_ps[0][:].rearrange("p (a j) -> p a j", a=OS),
                                     ACT.Copy).then_inc(aT_kept_act, 1)
            iterations(act, body)

        @block.vector
        def _(dve):
            for p in range(PAIR):
                rows = slice(C * p, C * p + C)
                nc.vector.memset(bias_rows[rows, 1 - p, :], 0.0)
                last = nc.vector.memset(w_rows[rows, :, 1 - p, :], 0.0)
            last.then_inc(zeros_set, 1)
            nc.vector.memset(z_sb[:, GT, :], 0.0).then_inc(zeros_set, 1)
            dve.wait_ge(consts_set, 2)
            nc.vector.tensor_reduce(own_slice[:], ident[:].rearrange("p (q s) -> p s q", s=OS), AX.X, ALU.add).then_inc(dve_consts, 1)
            nc.vector.tensor_reduce(own_half[:], ident[:].rearrange("p (a c) -> p a c", a=PAIR), AX.X, ALU.add).then_inc(dve_consts, 1)
            dve.wait_ge(rT_done, 1)
            nc.vector.tensor_copy(rT_sb[:], rT_ps.rearrange("p (c e) -> p c e", c=HC)).then_inc(rT_kept, 1)
            dve.wait_ge(net_loaded[2], 32)
            dve.wait_ge(net_pe, 4)
            nc.vector.tensor_tensor(att_logits[:], att_ps, b2_sb[:], ALU.add).then_inc(net_dve, 1)
            dve.wait_ge(net_dve, 1)
            nc.vector.tensor_reduce(att_max[:], att_logits[:], AX.X, ALU.max).then_inc(net_dve, 1)
            dve.wait_ge(net_dve, 2)
            nc.vector.tensor_scalar(att_shifted[:], att_logits[:], att_max[:, 0:1], None, ALU.subtract).then_inc(net_dve, 1)
            dve.wait_ge(net_act, 4)
            nc.vector.tensor_reduce(att_total[:], att_exp[:], AX.X, ALU.add).then_inc(net_dve, 1)
            dve.wait_ge(net_dve, 4)
            nc.vector.reciprocal(att_inv[:], att_total[:]).then_inc(net_dve, 1)
            dve.wait_ge(net_dve, 5)
            nc.vector.tensor_scalar(att_wide[:].rearrange("b p k s -> b p (k s)").rearrange("b p (k s) -> b p k s", k=K),
                                    att_exp[:].unsqueeze(1).unsqueeze(3).to_broadcast([B, PAIR, K, OS]),
                                    att_inv[:, 0:1], None, ALU.mult).then_inc(net_dve, 1)
            dve.wait_ge(dve_consts, 1)
            dve.wait_ge(net_pe, 5)
            for p in range(PAIR):
                rows = slice(C * p, C * p + C)
                mine = attT_ps[rows].rearrange("r (j p) -> r p j", p=PAIR)[:, p, :]
                nc.vector.tensor_tensor(att_diag[rows], mine.unsqueeze(1).to_broadcast([C, OS, NJ]),
                                        own_slice[rows].unsqueeze(2).to_broadcast([C, OS, NJ]), ALU.mult).then_inc(net_dve, 1)
            dve.wait_ge(ab_done, 1)
            nc.vector.tensor_copy(ab_all[:], ab_ps).then_inc(ab_kept, 1)
            dve.wait_ge(r_sum_done, 1)
            nc.vector.tensor_copy(r_sum[:], r_sum_ps).then_inc(r_sum_kept, 1)
            for s in range(1, GS, 2):
                dve.wait_ge(aT_done, s + 1)
                nc.vector.tensor_copy(aT_slice(s), out_ps[1][:].rearrange("p (a j) -> p a j", a=OS)).then_inc(aT_kept_dve, 1)
            dve.wait_ge(aT_kept_act, GS // 2)
            dve.wait_ge(aT_kept_dve, GS // 2)
            for p in range(PAIR):
                nc.vector.tensor_copy(aT_top[:, :, p, :], aT_all[C * p:C * p + C]).then_inc(aT_top_ready, 1)
            dve.wait_ge(aT_top_ready, PAIR)
            dve.wait_ge(ab_kept, 1)

            def body(g, parity, n=None):
                _, routing, _ = stages(g, n)
                q = g - 1
                if not routing:
                    return

                def step(m):
                    dve.wait_ge(chain, STEPS * q + m)

                def copy_x(k):
                    s = (1 - parity) * GT + k
                    dve.wait_ge(x_loaded[s], 16 * loads(g, parity, n, older=1))
                    if n is not None or g >= 2:
                        dve.wait_ge(out_done, UNITS * (g - 2) + HH * (k + 1))
                    for p in range(PAIR):
                        last = nc.vector.tensor_copy(xe_sb[0:C, k, p, :], x_sb[C * p:C * p + C, s, :])
                    last.then_inc(xe_ready, 1)

                dve.wait_ge(logit_bias_ready, q + 1)
                dve.wait_ge(logits_done, q + 1)
                nc.vector.tensor_tensor(logits[:], logit_ps[:].rearrange("p (k n) -> p k n", k=GT)[:, :, 0:NE],
                                        logit_bias[:], ALU.add).then_inc(chain, 1)
                step(1)
                nc.vector.tensor_reduce(row_max[:], logits[:], AX.X, ALU.max).then_inc(chain, 1)
                step(2)
                nc.vector.tensor_tensor(shifted[:], logits[:], row_max[:].unsqueeze(2).to_broadcast([P, GT, NE]),
                                        ALU.subtract).then_inc(shifted_ready, 1)
                copy_x(0)
                dve.wait_ge(exp_ready, q + 1)
                nc.vector.tensor_reduce(exp_sum[:], expd[:], AX.X, ALU.add).then_inc(chain, 1)
                for k in range(GT):
                    last = nc.vector.max(top8[:, k, :], expd[:, k, :])
                last.then_inc(chain, 1)
                step(3)
                nc.vector.reciprocal(inv_sum[:], exp_sum[:]).then_inc(chain, 1)
                step(4)
                nc.vector.tensor_reduce(top_sum[:], top8[:], AX.X, ALU.add).then_inc(chain, 1)
                for k in range(GT):
                    last = nc.vector.match_replace(rest[:, k, :], top8[:, k, :], expd[:, k, :], 0.0)
                last.then_inc(chain, 1)
                step(6)
                nc.vector.tensor_tensor(w_sum[:], top_sum[:], inv_sum[:], ALU.mult).then_inc(chain, 1)
                step(7)
                nc.vector.tensor_tensor(kept[:], expd[:], rest[:], ALU.subtract).then_inc(chain, 1)
                if n is not None or q >= 1:
                    dve.wait_ge(mixT_done, q)
                step(8)
                nc.vector.tensor_copy(mix[:, :, 0:C], w_sum[:].unsqueeze(2).to_broadcast([P, GT, C]))
                nc.vector.tensor_tensor(out_bias[:, 1 - parity, :], w_sum[:], ab_all[:, bass.ds(GT * q, GT)],
                                        ALU.mult).then_inc(out_bias_ready, 1)
                step(9)
                nc.vector.tensor_tensor(mix[:, :, C:C + NE], kept[:], inv_sum[:].unsqueeze(2).to_broadcast([P, GT, NE]),
                                        ALU.mult).then_inc(mix_ready, 1)
                for k in range(1, GT):
                    copy_x(k)
                dve.wait_ge(mixT_done, q + 1)
                nc.vector.tensor_tensor(mixT_sb[0:C].rearrange("p k (a o) -> p (k a) o", a=PAIR),
                                        mixT_ps[0:C, :].rearrange("p (k o) -> p k o", k=GT * PAIR),
                                        aT_top[:, bass.ds(GT * q, GT), :, :].rearrange("p k a o -> p (k a) o"),
                                        ALU.mult).then_inc(mixT_scaled, 1)
                dve.wait_ge(mixT_scaled, q + 1)
                nc.vector.tensor_tensor(mixT_sb[0:C].rearrange("p k (a o) -> p (k a) o", a=PAIR),
                                        mixT_sb[0:C].rearrange("p k (a o) -> p (k a) o", a=PAIR),
                                        ident[0:C, 0:C].unsqueeze(1).to_broadcast([C, GT * PAIR, C]),
                                        ALU.add).then_inc(mixT_x_ready, 1)

            iterations(dve, body)

        @block.tensor
        def _(pe):
            def transpose_x(g, parity, u, x_loads, n=None):
                k, h = u // HH, u % HH
                if h == 0:
                    pe.wait_ge(x_loaded[parity * GT + k], 16 * x_loads)
                if n is not None or UNITS * g + u >= HH:
                    pe.wait_ge(xT_kept, UNITS * g + u - HH + 1)
                for c in range(CU):
                    last = nc.tensor.transpose(xT_ps[h][:, P * c:P * c + P],
                                               x_sb[:, parity * GT + k, P * (CU * h + c):P * (CU * h + c + 1)], ident[:])
                last.then_inc(xT_done, 1)

            def make_zT(g, chunks):
                pe.wait_ge(xT_kept, UNITS * g + UNITS)
                for c in chunks:
                    for s in range(2):
                        last = nc.tensor.matmul(zT_ps[NE * s:NE * s + NE, 0:PAIR * P], rT_sb[:, c, :],
                                                xT_sb[:, c, PAIR * P * s:PAIR * P * (s + 1)], start=(c == 0), stop=(c == HC - 1))
                if c == HC - 1:
                    last.then_inc(zT_done, 1)

            def make_z(g):
                pe.wait_ge(zT_kept, g)
                for m in range(2):
                    last = nc.tensor.transpose(z_ps[:, P * m:P * m + P], zT_sb[:, P * m:P * m + P], ident[:])
                last.then_inc(z_done, 1)

            def make_logits(g):
                pe.wait_ge(blocks_ready, g)
                pe.wait_ge(z_kept, g)
                for k in range(GT):
                    m = 2 * (k % 2) + k // 2
                    last = nc.tensor.matmul(logit_ps[:, P * k:P * k + P], at_blocks[:, k, :],
                                            z_sb[:, m:m + 2, :].rearrange("p m e -> p (m e)"), start=True, stop=True)
                last.then_inc(logits_done, 1)

            def make_mixT(g):
                pe.wait_ge(mix_ready, g)
                for k in range(GT):
                    last = nc.tensor.transpose(mixT_ps[:, P * k:P * k + P], mix[:, k, :], ident[:])
                last.then_inc(mixT_done, 1)

            def make_out(g, u, n):
                q, k, h = g - 2, u // HH, u % HH
                if u == 0:
                    pe.wait_ge(mixT_x_ready, q + 1)
                    pe.wait_ge(mixT_e_ready, q + 1)
                if h == 0:
                    pe.wait_ge(xe_ready, GT * q + k + 1)
                if n is not None or UNITS * q + u >= HH:
                    pe.wait_ge(out_kept, UNITS * q + u - HH + 1)
                for p in range(PAIR):
                    last = nc.tensor.matmul(out_ps[h][C * p:C * p + C, :], mixT_sb[:, k, C * p:C * p + C],
                                            xe_sb[:, k, p, BANK * h:BANK * h + BANK], start=True, stop=True)
                last.then_inc(out_done, 1)

            def body(g, parity, n=None):
                transposing, routing, putting_out = stages(g, n)
                x_loads = loads(g, parity, n)
                if routing and not transposing:
                    make_z(g)
                    make_logits(g)
                for u in range(UNITS + 1):
                    if transposing and u < UNITS:
                        transpose_x(g, parity, u, x_loads, n)
                    if routing and transposing and u == 1:
                        make_z(g)
                    if putting_out and u >= 1:
                        make_out(g, u - 1, n)
                    if routing and transposing and u == 2:
                        make_logits(g)
                if transposing:
                    make_zT(g, range(0, HC // 2))
                if routing:
                    make_mixT(g)
                if transposing:
                    make_zT(g, range(HC // 2, HC))

            pe.wait_ge(consts_set, 2)
            pe.wait_ge(net_loaded[0], 48)
            nc.tensor.transpose(condT_ps, cond_sb[:], ident[:]).then_inc(net_pe, 1)
            pe.wait_ge(net_act, 1)
            nc.tensor.matmul(h1_ps, w0_sb[:], condT_sb[:], start=True, stop=True).then_inc(net_pe, 1)
            pe.wait_ge(router_loaded, 32)
            for c in range(HC):
                last = nc.tensor.transpose(rT_ps[:, NE * c:NE * c + NE], router_sb[:, P * c:P * c + P], ident[0:NE, 0:NE])
            last.then_inc(rT_done, 1)
            pe.wait_ge(net_loaded[1], 32)
            pe.wait_ge(net_act, 2)
            nc.tensor.matmul(h2_ps, w1_sb[:], h1T_sb[:], start=True, stop=True).then_inc(net_pe, 1)
            for u in range(0, 2):
                transpose_x(0, 0, u, 1)
            pe.wait_ge(net_loaded[2], 32)
            pe.wait_ge(net_act, 3)
            nc.tensor.matmul(att_ps, h2T_sb[:], w2_sb[:], start=True, stop=True).then_inc(net_pe, 1)
            for u in range(2, 6):
                transpose_x(0, 0, u, 1)
            pe.wait_ge(net_dve, 6)
            nc.tensor.transpose(attT_ps, att_wide[:].rearrange("b p k s -> b (p k s)"), ident[:]).then_inc(net_pe, 1)
            for u in range(6, UNITS):
                transpose_x(0, 0, u, 1)
            pe.wait_ge(net_dve, 8)
            pe.wait_ge(mats_loaded, 16 * 2 * PAIR)
            nc.tensor.matmul(ab_ps, bias_rows[:].rearrange("p a o -> p (a o)"), att_diag[:, 0, :], start=True, stop=True).then_inc(ab_done, 1)
            pe.wait_ge(rT_kept, 1)
            pe.wait_ge(consts_set, 3)
            for c in range(HC):
                last = nc.tensor.matmul(r_sum_ps, ones[:], rT_sb[:, c, :], start=(c == 0), stop=(c == HC - 1))
            last.then_inc(r_sum_done, 1)
            pe.wait_ge(r_sum_kept, 1)
            for s in range(GS):
                if s >= 2:
                    pe.wait_ge((aT_kept_act, aT_kept_dve)[s % 2], s // 2)
                nc.tensor.matmul(out_ps[s % 2][:], w_rows[:, s, :, :].rearrange("p a i -> p (a i)"),
                                 att_diag[:].rearrange("p a j -> p (a j)"), start=True, stop=True).then_inc(aT_done, 1)
            make_zT(0, range(HC))
            pe.wait_ge(aT_kept_act, GS // 2)
            pe.wait_ge(aT_kept_dve, GS // 2)
            pe.wait_ge(zeros_set, 2)
            pe.wait_ge(experts_loaded, 16 * GT * PAIR)

            iterations(pe, body)


_INS = ['x', 'cond_128', 'L0_cond_W0', 'L0_cond_b0', 'L0_cond_W1', 'L0_cond_b1', 'L0_cond_W2', 'L0_cond_b2',
        'L0_cond_weight', 'L0_cond_bias_k', 'L0_ffn_router_weight', 'L0_ffn_router_bias', 'L0_ffn_expert_bias']
_OUTS = [((B, C, H), 'float32')]


def kernel(**inputs):
    import numpy as _np
    import concourse.bacc as _bacc
    from concourse import mybir as _mybir
    from concourse.bass_utils import run_bass_kernel_spmd as _run

    nc = _bacc.Bacc("TRN2", target_bir_lowering=False, num_devices=1)
    arrays, args = {}, []
    for name in _INS:
        a = _np.ascontiguousarray(inputs[name])
        arrays[f"in_{name}_dram"] = a
        args.append(nc.dram_tensor(f"in_{name}_dram", a.shape, _mybir.dt.from_np(a.dtype), kind="ExternalInput").ap())
    for i, (shape, dtype) in enumerate(_OUTS):
        dt = _mybir.dt.from_np(_np.dtype(dtype))
        args.append(nc.dram_tensor(f"out_{i}_dram", shape, dt, kind="ExternalOutput").ap())
    adaln_ffn_kernel(nc, *args)
    r = _run(nc, [arrays], core_ids=[0])
    got = tuple(r.results[0][f"out_{i}_dram"] for i in range(len(_OUTS)))
    return got[0]
```

```python
import concourse.bass as bass
from concourse import mybir
from contextlib import ExitStack
import itertools

FP32 = mybir.dt.float32
ALU = mybir.AluOpType
ACT = mybir.ActivationFunctionType
AX = mybir.AxisListType

P = 128
Q = 32
B, C, H = 128, 64, 1024
K = 8
NE = 64
TOP = 8
D = 128
PAIR = P // C
NJ = B // PAIR
GT = 4
NG = NJ // GT
TILE = P * H
HC = H // P
BANK = 512
HH = H // BANK
UNITS = GT * HH
CU = BANK // P
OS = 8
GS = C // OS
SLOTS = 2 * GT
STEADY = 4
LN = 96
AHEAD = 2
STEPS = 10


def adaln_ffn_kernel(nc, x, cond, w0, b0, w1, b1, w2, b2, weight, bias_k, router, router_bias, expert_bias, out):
    x_tiles = x.rearrange("b c h -> (b c) h").rearrange("(j p) h -> j p h", p=P)
    x_flat, out_flat = x.rearrange("b c h -> (b c h)"), out.rearrange("b c h -> (b c h)")
    w_koi = weight.rearrange("k o i u -> k o (i u)")

    def tile_at(flat, start):
        return flat[bass.ds(start, TILE)].rearrange("(p h) -> p h", p=P)

    ctx = ExitStack()
    with ctx:
        def sb(name, shape):
            return ctx.enter_context(nc.sbuf_tensor(name, shape, FP32))

        def bank(name):
            return ctx.enter_context(nc.psum_tensor(name, [P, BANK], FP32))

        def sem(name):
            return ctx.enter_context(nc.semaphore(name))

        x_sb = sb("x_sb", [P, SLOTS, H])
        xe_sb = sb("xe_sb", [P, GT, PAIR, H])
        xT_sb = sb("xT_sb", [P, HC, GT * P])
        out_sb = sb("out_sb", [P, GT, H])
        zT_sb = sb("zT_sb", [P, PAIR * P])
        z_sb = sb("z_sb", [P, GT + 1, NE])
        at_blocks = sb("at_blocks", [P, GT, P])
        logit_bias = sb("logit_bias", [P, GT, NE])
        logits = sb("logits", [P, GT, NE])
        shifted = sb("shifted", [P, GT, NE])
        expd = sb("expd", [P, GT, NE])
        rest = sb("rest", [P, GT, NE])
        kept = sb("kept", [P, GT, NE])
        row_max = sb("row_max", [P, GT])
        top8 = sb("top8", [P, GT, TOP])
        sums = sb("sums", [P, 2, GT])
        inv_sums = sb("inv_sums", [P, 2, GT])
        w_sum = sb("w_sum", [P, 2, GT])
        out_bias = sb("out_bias", [P, 2, GT])
        w_inv_top = sb("w_inv_top", [C, GT, PAIR])
        diagonals = sb("diagonals", [C, GT, PAIR, C])
        shares = sb("shares", [P, GT, NE])
        mixT_sb = sb("mixT_sb", [P, 2, GT, P])
        aT_all = sb("aT_all", [P, NJ, C])
        aT_top = sb("aT_top", [C, NJ, PAIR, C])
        ab_all = sb("ab_all", [P, NJ])
        rT_sb = sb("rT_sb", [P, HC, NE])
        r_sum = sb("r_sum", [P, NE])
        rb_sb = sb("rb_sb", [P, NE])
        ident = sb("ident", [P, P])
        ones = sb("ones", [P, P])
        act_warm = sb("act_warm", [P, 1])
        own_half = sb("own_half", [P, PAIR])
        own_slice = sb("own_slice", [P, OS])
        cond_sb = sb("cond_sb", [B, D])
        condT_sb = sb("condT_sb", [D, B])
        w0_sb, w1_sb, w2_sb = sb("w0_sb", [D, D]), sb("w1_sb", [D, D]), sb("w2_sb", [D, K])
        b0_sb, b1_sb, b2_sb = sb("b0_sb", [D, 1]), sb("b1_sb", [D, 1]), sb("b2_sb", [B, K])
        h1T_sb, h2T_sb = sb("h1T_sb", [D, B]), sb("h2T_sb", [D, B])
        att_logits, att_shifted, att_exp = sb("att_logits", [B, K]), sb("att_shifted", [B, K]), sb("att_exp", [B, K])
        att_max, att_total, att_inv = sb("att_max", [B, 1]), sb("att_total", [B, 1]), sb("att_inv", [B, 1])
        att_wide = sb("att_wide", [B, PAIR, K, OS])
        att_diag = sb("att_diag", [P, OS, NJ])
        router_sb = sb("router_sb", [NE, H])
        w_rows = sb("w_rows", [P, GS, PAIR, C])
        bias_rows = sb("bias_rows", [P, PAIR, C])

        xT_ps = [bank("xT_ps0"), bank("xT_ps1")]
        out_ps = [bank("out_ps0"), bank("out_ps1")]
        zT_ps, z_ps, logit_ps, net_ps = bank("zT_ps"), bank("z_ps"), bank("logit_ps"), bank("net_ps")
        condT_ps, h1_ps, h2_ps, att_ps = net_ps[:, 0:B], net_ps[:, B:2 * B], net_ps[:, 2 * B:3 * B], net_ps[:, 3 * B:3 * B + K]
        rT_ps, r_sum_ps = z_ps[:, 0:HC * NE], z_ps[:, 0:HC * NE]
        attT_ps, ab_ps = logit_ps[:, 0:B], logit_ps[:, B:B + NJ]

        net_loaded = [sem(f"net_loaded{layer}") for layer in range(3)]
        mats_loaded = sem("mats_loaded")
        router_loaded = sem("router_loaded")
        experts_loaded = sem("experts_loaded")
        x_loaded = [sem(f"x_loaded{s}") for s in range(SLOTS)]
        stored = [sem(f"stored{k}") for k in range(GT)]
        consts_set = sem("consts_set")
        zeros_set = sem("zeros_set")
        net_pe = sem("net_pe")
        net_act = sem("net_act")
        net_dve = sem("net_dve")
        rT_done, rT_kept = sem("rT_done"), sem("rT_kept")
        r_sum_done, r_sum_kept = sem("r_sum_done"), sem("r_sum_kept")
        dve_consts = sem("dve_consts")
        ab_done, ab_kept = sem("ab_done"), sem("ab_kept")
        aT_done = sem("aT_done")
        aT_kept_act, aT_kept_dve = sem("aT_kept_act"), sem("aT_kept_dve")
        aT_top_ready = sem("aT_top_ready")
        xT_done, xT_kept = sem("xT_done"), sem("xT_kept")
        zT_done, zT_kept = sem("zT_done"), sem("zT_kept")
        z_done, z_kept = sem("z_done"), sem("z_kept")
        logits_done = sem("logits_done")
        blocks_ready, logit_bias_ready = sem("blocks_ready"), sem("logit_bias_ready")
        shifted_ready, exp_ready = sem("shifted_ready"), sem("exp_ready")
        out_bias_ready = sem("out_bias_ready")
        w_inv_ready, diagonals_ready = sem("w_inv_ready"), sem("diagonals_ready")
        mixT_ready = sem("mixT_ready")
        chain = sem("chain")
        logit_bias_scaled = sem("logit_bias_scaled")
        xe_ready = sem("xe_ready")
        out_done = sem("out_done")
        out_kept = sem("out_kept")

        def iterations(eng, body, first=1, last=NG):
            for g in range(first, STEADY):
                body(g, g % 2)
            with eng.Fori(0, (last - STEADY) // 2) as n:
                for parity in range(2):
                    body(2 * n + (STEADY + parity), parity, n)
            for g in range(last, NG + 2):
                body(g, g % 2)

        def loads(g, parity, n, older=0):
            return (g - older) // 2 + 1 if n is None else n + STEADY // 2 + 1 - (older if parity == 0 else 0)

        def stages(g, n):
            return (True, True, True) if n is not None else (g < NG, 1 <= g <= NG, 2 <= g)

        def xT_bank(g, u, n=None):
            if n is None and g == 1:
                return (xT_ps + out_ps)[u % 4], 2 if u < 2 else 4
            return xT_ps[u % 2], 2

        def out_bank(g, u, n=None):
            if n is None and g >= NG:
                return (out_ps + xT_ps)[u % 4], 2 if g == NG and u < 2 else 4
            return out_ps[u % 2], 2

        def aT_slice(s):
            return aT_all[:].rearrange("p j (a s) -> p a j s", s=GS)[:, :, :, s]

        block = ctx.enter_context(nc.Block())

        @block.sync
        def _(sp):
            def load_x(s):
                sp.dma_start(x_sb[:, s, :], x_tiles[s]).then_inc(x_loaded[s], 16)

            sp.dma_start(cond_sb[:], cond).then_inc(net_loaded[0], 16)
            sp.dma_start(w0_sb[:], w0).then_inc(net_loaded[0], 16)
            sp.dma_start(b0_sb[:], b0.unsqueeze(1)).then_inc(net_loaded[0], 16)
            sp.dma_start(w1_sb[:], w1).then_inc(net_loaded[1], 16)
            sp.dma_start(b1_sb[:], b1.unsqueeze(1)).then_inc(net_loaded[1], 16)
            sp.dma_start(w2_sb[:], w2).then_inc(net_loaded[2], 16)
            sp.dma_start(b2_sb[:], b2.partition_broadcast(B)).then_inc(net_loaded[2], 16)
            load_x(0)
            sp.dma_start(router_sb[:], router).then_inc(router_loaded, 16)
            sp.dma_start(rb_sb[:], router_bias.partition_broadcast(P)).then_inc(router_loaded, 16)
            for s in range(1, SLOTS):
                load_x(s)
            for k in range(GT):
                for p in range(PAIR):
                    sp.dma_start(xe_sb[C:P, k, p, :], expert_bias).then_inc(experts_loaded, 16)

            names = itertools.count()

            def early(value):
                register = sp.alloc_register(f"early{next(names)}")
                sp.reg_mov(register, value)
                return sp.snap(register, min_val=0, max_val=UNITS * NG)

            def body(g, parity, n=None):
                transposing, _, putting_out = stages(g, n)
                load_at = [GT * TILE * (g + 1) + TILE * k for k in range(GT)]
                store_at = [GT * TILE * (g - 2) + TILE * k for k in range(GT)]
                slot_free = [GT * (g - 1) + k + 1 for k in range(GT)]
                kept = [UNITS * (g - 2) + HH * (k + 1) for k in range(GT)]
                if n is not None:
                    kept = [early(v) for v in kept]
                for k in range(GT):
                    if n is not None or (transposing and 1 <= g <= NG - 2):
                        s = (1 - parity) * GT + k
                        sp.wait_ge(xe_ready, slot_free[k])
                        if n is None and g == 1:
                            sp.wait_ge(xT_done, HH * (k + 1))
                        sp.dma_start(x_sb[:, s, :], tile_at(x_flat, load_at[k])).then_inc(x_loaded[s], 16)
                    if putting_out:
                        if n is None and g == NG + 1 and k == GT - 1:
                            halves = tile_at(out_flat, store_at[k]).rearrange("p (h n) -> h p n", h=HH)
                            for h in range(HH):
                                sp.wait_ge(out_kept, kept[k] - HH + h + 1)
                                sp.dma_start(halves[h], out_sb[:, k, BANK * h:BANK * h + BANK]).then_inc(stored[k], 16)
                            continue
                        sp.wait_ge(out_kept, kept[k])
                        sp.dma_start(tile_at(out_flat, store_at[k]), out_sb[:, k, :]).then_inc(stored[k], 16)

            iterations(sp, body, last=NG - 2)
            for k in range(GT):
                sp.wait_ge(stored[k], 16 * (NG + (HH - 1 if k == GT - 1 else 0)))

        @block.gpsimd
        def _(pool):
            pool.memset(ident[:], 0.0).then_inc(consts_set, 1)
            pool.wait_ge(consts_set, 1)
            pool.affine_select(out=ident[:], in_=ident[:], compare_op=ALU.not_equal, fill=1.0, base=0,
                               pattern=[[-1, P]], channel_multiplier=1).then_inc(consts_set, 1)
            pool.memset(ones[:], 1.0).then_inc(consts_set, 1)
            pool.wait_ge(zeros_set, 1)
            for p in range(PAIR):
                rows = slice(C * p, C * p + C)
                pool.dma_start(w_rows[rows, :, p, :], w_koi.rearrange("k (s g) i -> (k s) g i", g=GS)).then_inc(mats_loaded, 16)
                pool.dma_start(bias_rows[rows, p, :],
                               bias_k.unsqueeze(1).to_broadcast([K, OS, C])).then_inc(mats_loaded, 16)
            pool.wait_ge(r_sum_kept, 1)
            pool.wait_ge(router_loaded, 32)
            pool.wait_ge(ab_kept, 1)
            pool.wait_ge(aT_kept_act, GS // 2)
            pool.wait_ge(aT_kept_dve, GS // 2)
            pool.wait_ge(dve_consts, 2)

            def body(g, parity, n=None):
                _, routing, _ = stages(g, n)
                if not routing:
                    return
                q = g - 1
                if n is not None or q >= 1:
                    pool.wait_ge(logits_done, q)
                pool.tensor_tensor(at_blocks[:].rearrange("p k (a c) -> p k a c", a=PAIR),
                                   aT_all[:, bass.ds(GT * q, GT), :].unsqueeze(2).to_broadcast([P, GT, PAIR, C]),
                                   own_half[:].unsqueeze(1).unsqueeze(3).to_broadcast([P, GT, PAIR, C]),
                                   ALU.mult).then_inc(blocks_ready, 1)
                if n is not None or q >= 1:
                    pool.wait_ge(shifted_ready, q)
                pool.tensor_tensor(logit_bias[:], ab_all[:, bass.ds(GT * q, GT)].unsqueeze(2).to_broadcast([P, GT, NE]),
                                   r_sum[:].unsqueeze(1).to_broadcast([P, GT, NE]), ALU.mult).then_inc(logit_bias_scaled, 1)
                pool.wait_ge(logit_bias_scaled, q + 1)
                pool.tensor_tensor(logit_bias[:], logit_bias[:], rb_sb[:].unsqueeze(1).to_broadcast([P, GT, NE]),
                                   ALU.add).then_inc(logit_bias_ready, 1)
                pool.wait_ge(w_inv_ready, q + 1)
                if n is not None or q >= 1:
                    pool.wait_ge(mixT_ready, q)
                pool.tensor_tensor(diagonals[:].rearrange("i k a o -> i (k a) o"),
                                   ident[0:C, 0:C].unsqueeze(1).to_broadcast([C, GT * PAIR, C]),
                                   w_inv_top[:].rearrange("i k a -> i (k a)").unsqueeze(2).to_broadcast([C, GT * PAIR, C]),
                                   ALU.mult).then_inc(diagonals_ready, 1)

            iterations(pool, body)

        @block.scalar
        def _(act):
            def keep_xT(g, u, n=None):
                act.wait_ge(xT_done, UNITS * g + u + 1)
                k, h = u // HH, u % HH
                nc.scalar.activation(xT_sb[:, CU * h:CU * h + CU, P * k:P * k + P],
                                     xT_bank(g, u, n)[0][:].rearrange("p (c t) -> p c t", c=CU), ACT.Copy).then_inc(xT_kept, 1)

            def keep_out(g, parity, u, n):
                q, k, h = g - 2, u // HH, u % HH
                if h == 0 and (n is not None or q >= 1):
                    act.wait_ge(stored[k], 16 * q)
                if u == 0:
                    act.wait_ge(out_bias_ready, q + 1)
                act.wait_ge(out_done, UNITS * q + u + 1)
                nc.scalar.activation(out_sb[:, k, BANK * h:BANK * h + BANK], out_bank(g, u, n)[0][:], ACT.Identity,
                                     bias=out_bias[:, parity, k:k + 1], scale=w_sum[:, parity, k:k + 1]).then_inc(out_kept, 1)

            def keep_z(g):
                act.wait_ge(z_done, g)
                nc.scalar.activation(z_sb[:, 0:GT, :], z_ps[:, 0:GT * NE].rearrange("p (m e) -> p m e", m=GT),
                                     ACT.Copy).then_inc(z_kept, 1)

            def keep_zT(g):
                act.wait_ge(zT_done, g)
                nc.scalar.activation(zT_sb[:], zT_ps[:, 0:PAIR * P], ACT.Copy).then_inc(zT_kept, 1)

            def exponentials(g):
                act.wait_ge(shifted_ready, g)
                nc.scalar.activation(expd[:], shifted[:], ACT.Exp).then_inc(exp_ready, 1)

            def body(g, parity, n=None):
                transposing, routing, putting_out = stages(g, n)
                ahead = AHEAD if n is None and g == 2 else 0
                if routing and not ahead:
                    keep_zT(g)
                for u in range(UNITS + 1):
                    if transposing and ahead <= u < UNITS:
                        keep_xT(g, u, n)
                    if routing and u == 1:
                        keep_z(g)
                    if putting_out and u >= 1:
                        keep_out(g, parity, u - 1, n)
                    if routing and u == 2:
                        exponentials(g)

            act.wait_ge(consts_set, 3)
            nc.scalar.activation(act_warm[:], ones[:, 0:1], ACT.Gelu)
            act.wait_ge(net_pe, 1)
            nc.scalar.activation(condT_sb[:], condT_ps, ACT.Copy).then_inc(net_act, 1)
            act.wait_ge(net_loaded[0], 48)
            act.wait_ge(net_pe, 2)
            nc.scalar.activation(h1T_sb[:], h1_ps, ACT.Gelu, bias=b0_sb[:, 0:1]).then_inc(net_act, 1)
            act.wait_ge(net_loaded[1], 32)
            act.wait_ge(net_pe, 3)
            nc.scalar.activation(h2T_sb[:], h2_ps, ACT.Gelu, bias=b1_sb[:, 0:1]).then_inc(net_act, 1)
            nc.scalar.activation(act_warm[:], ones[:, 0:1], ACT.Exp)
            act.wait_ge(net_dve, 3)
            nc.scalar.activation(att_exp[:], att_shifted[:], ACT.Exp).then_inc(net_act, 1)
            for u in range(0, 2 * HH):
                keep_xT(0, u)
            for s in range(GS):
                if s % 2 == 0:
                    act.wait_ge(aT_done, s + 1)
                    nc.scalar.activation(aT_slice(s), out_ps[0][:].rearrange("p (a j) -> p a j", a=OS),
                                         ACT.Copy).then_inc(aT_kept_act, 1)
                if s + 2 * HH < UNITS:
                    keep_xT(0, s + 2 * HH)
            keep_zT(1)
            for u in range(UNITS):
                keep_xT(1, u)
                if u == 1:
                    keep_z(1)
            exponentials(1)
            keep_zT(2)
            for u in range(AHEAD):
                keep_xT(2, u)
            iterations(act, body, first=2)

        @block.vector
        def _(dve):
            def copy_x(q, parity, k, x_loads):
                s = parity * GT + k
                dve.wait_ge(x_loaded[s], 16 * x_loads)
                if type(q) is not int or q >= 1:
                    dve.wait_ge(out_done, UNITS * (q - 1) + HH * (k + 1))
                for p in range(PAIR):
                    last = nc.vector.tensor_copy(xe_sb[0:C, k, p, :], x_sb[C * p:C * p + C, s, :])
                last.then_inc(xe_ready, 1)

            for p in range(PAIR):
                rows = slice(C * p, C * p + C)
                nc.vector.memset(bias_rows[rows, 1 - p, :], 0.0)
                last = nc.vector.memset(w_rows[rows, :, 1 - p, :], 0.0)
            last.then_inc(zeros_set, 1)
            nc.vector.memset(z_sb[:, GT, :], 0.0).then_inc(zeros_set, 1)
            dve.wait_ge(consts_set, 2)
            nc.vector.tensor_reduce(own_slice[:], ident[:].rearrange("p (q s) -> p s q", s=OS), AX.X, ALU.add).then_inc(dve_consts, 1)
            nc.vector.tensor_reduce(own_half[:], ident[:].rearrange("p (a c) -> p a c", a=PAIR), AX.X, ALU.add).then_inc(dve_consts, 1)
            dve.wait_ge(net_loaded[2], 32)
            dve.wait_ge(net_pe, 4)
            nc.vector.tensor_tensor(att_logits[:], att_ps, b2_sb[:], ALU.add).then_inc(net_dve, 1)
            dve.wait_ge(net_dve, 1)
            nc.vector.tensor_reduce(att_max[:], att_logits[:], AX.X, ALU.max).then_inc(net_dve, 1)
            dve.wait_ge(net_dve, 2)
            nc.vector.tensor_scalar(att_shifted[:], att_logits[:], att_max[:, 0:1], None, ALU.subtract).then_inc(net_dve, 1)
            dve.wait_ge(net_act, 4)
            nc.vector.tensor_reduce(att_total[:], att_exp[:], AX.X, ALU.add).then_inc(net_dve, 1)
            dve.wait_ge(net_dve, 4)
            nc.vector.reciprocal(att_inv[:], att_total[:]).then_inc(net_dve, 1)
            dve.wait_ge(net_dve, 5)
            nc.vector.tensor_scalar(att_wide[:].rearrange("b p k s -> b p (k s)").rearrange("b p (k s) -> b p k s", k=K),
                                    att_exp[:].unsqueeze(1).unsqueeze(3).to_broadcast([B, PAIR, K, OS]),
                                    att_inv[:, 0:1], None, ALU.mult).then_inc(net_dve, 1)
            dve.wait_ge(dve_consts, 1)
            dve.wait_ge(net_pe, 5)
            for p in range(PAIR):
                rows = slice(C * p, C * p + C)
                mine = attT_ps[rows].rearrange("r (j p) -> r p j", p=PAIR)[:, p, :]
                nc.vector.tensor_tensor(att_diag[rows], mine.unsqueeze(1).to_broadcast([C, OS, NJ]),
                                        own_slice[rows].unsqueeze(2).to_broadcast([C, OS, NJ]), ALU.mult).then_inc(net_dve, 1)
            dve.wait_ge(rT_done, 1)
            nc.vector.tensor_copy(rT_sb[:], rT_ps.rearrange("p (c e) -> p c e", c=HC)).then_inc(rT_kept, 1)
            dve.wait_ge(ab_done, 1)
            nc.vector.tensor_copy(ab_all[:], ab_ps).then_inc(ab_kept, 1)
            for s in range(1, GS, 2):
                dve.wait_ge(aT_done, s + 1)
                nc.vector.tensor_copy(aT_slice(s), out_ps[1][:].rearrange("p (a j) -> p a j", a=OS)).then_inc(aT_kept_dve, 1)
                copy_x(0, 0, s // 2, 1)
            dve.wait_ge(r_sum_done, 1)
            nc.vector.tensor_reduce(r_sum[:], r_sum_ps.rearrange("p (c e) -> p e c", c=HC), AX.X, ALU.add).then_inc(r_sum_kept, 1)
            dve.wait_ge(aT_kept_act, GS // 2)
            dve.wait_ge(aT_kept_dve, GS // 2)
            for p in range(PAIR):
                nc.vector.tensor_copy(aT_top[:, :, p, :], aT_all[C * p:C * p + C]).then_inc(aT_top_ready, 1)
            dve.wait_ge(aT_top_ready, PAIR)
            dve.wait_ge(ab_kept, 1)

            def body(g, parity, n=None):
                transposing, routing, putting_out = stages(g, n)
                if not routing:
                    return
                q, q_parity, q_loads = g - 1, 1 - parity, loads(g, parity, n, older=1)

                def step(m):
                    dve.wait_ge(chain, STEPS * q + m)

                dve.wait_ge(logit_bias_ready, q + 1)
                dve.wait_ge(logits_done, q + 1)
                nc.vector.tensor_tensor(logits[:], logit_ps[:].rearrange("p (k n) -> p k n", k=GT)[:, :, 0:NE],
                                        logit_bias[:], ALU.add).then_inc(chain, 1)
                step(1)
                nc.vector.tensor_reduce(row_max[:], logits[:], AX.X, ALU.max).then_inc(chain, 1)
                step(2)
                nc.vector.tensor_tensor(shifted[:], logits[:], row_max[:].unsqueeze(2).to_broadcast([P, GT, NE]),
                                        ALU.subtract).then_inc(shifted_ready, 1)
                if putting_out:
                    copy_x(q, q_parity, 0, q_loads)
                dve.wait_ge(exp_ready, q + 1)
                nc.vector.tensor_reduce(sums[:, 0, :], expd[:], AX.X, ALU.add).then_inc(chain, 1)
                for k in range(GT):
                    last = nc.vector.max(top8[:, k, :], expd[:, k, :])
                last.then_inc(chain, 1)
                step(4)
                nc.vector.tensor_reduce(sums[:, 1, :], top8[:], AX.X, ALU.add).then_inc(chain, 1)
                for k in range(GT):
                    last = nc.vector.match_replace(rest[:, k, :], top8[:, k, :], expd[:, k, :], 0.0)
                last.then_inc(chain, 1)
                step(5)
                nc.vector.reciprocal(inv_sums[:], sums[:]).then_inc(chain, 1)
                step(6)
                nc.vector.tensor_tensor(kept[:], expd[:], rest[:], ALU.subtract).then_inc(chain, 1)
                step(7)
                for p in range(PAIR):
                    rows = slice(C * p, C * p + C)
                    last = nc.vector.tensor_tensor(w_inv_top[:, :, p], sums[rows, 0, :], inv_sums[rows, 1, :], ALU.mult)
                last.then_inc(w_inv_ready, 1)
                nc.vector.tensor_tensor(w_sum[:, q_parity, :], sums[:, 1, :], inv_sums[:, 0, :], ALU.mult).then_inc(chain, 1)
                step(8)
                nc.vector.tensor_tensor(shares[:], kept[:], inv_sums[:, 1, :].unsqueeze(2).to_broadcast([P, GT, NE]),
                                        ALU.mult).then_inc(chain, 1)
                step(9)
                nc.vector.tensor_tensor(out_bias[:, q_parity, :], w_sum[:, q_parity, :], ab_all[:, bass.ds(GT * q, GT)],
                                        ALU.mult).then_inc(out_bias_ready, 1)
                early = range(1, GT - 1) if transposing and putting_out else range(0)
                late = range(GT - 1 if transposing else 1, GT) if putting_out else range(0)
                for k in early:
                    copy_x(q, q_parity, k, q_loads)
                step(10)
                for row in range(0, P, Q):
                    for col in range(0, NE, Q):
                        nc.vector.transpose(mixT_sb[C + col:C + col + Q, q_parity, :, row:row + Q],
                                            shares[row:row + Q, :, col:col + Q])
                dve.wait_ge(diagonals_ready, q + 1)
                nc.vector.tensor_tensor(mixT_sb[0:C, q_parity].rearrange("i k r -> i (k r)"),
                                        aT_top[:, bass.ds(GT * q, GT), :, :].rearrange("i k a o -> i (k a o)"),
                                        diagonals[:].rearrange("i k a o -> i (k a o)"), ALU.add).then_inc(mixT_ready, 1)
                for k in late:
                    copy_x(q, q_parity, k, q_loads)

            iterations(dve, body)

        @block.tensor
        def _(pe):
            def transpose_x(g, parity, u, x_loads, n=None):
                k, h = u // HH, u % HH
                if h == 0:
                    pe.wait_ge(x_loaded[parity * GT + k], 16 * x_loads)
                to, back = xT_bank(g, u, n)
                if n is not None or UNITS * g + u >= back:
                    pe.wait_ge(xT_kept, UNITS * g + u - back + 1)
                for c in range(CU):
                    last = nc.tensor.transpose(to[:, P * c:P * c + P],
                                               x_sb[:, parity * GT + k, P * (CU * h + c):P * (CU * h + c + 1)], ident[:])
                last.then_inc(xT_done, 1)

            def make_zT(g):
                pe.wait_ge(xT_kept, UNITS * g + UNITS)
                for c in range(HC):
                    for s in range(2):
                        last = nc.tensor.matmul(zT_ps[NE * s:NE * s + NE, 0:PAIR * P], rT_sb[:, c, :],
                                                xT_sb[:, c, PAIR * P * s:PAIR * P * (s + 1)], start=(c == 0), stop=(c == HC - 1))
                last.then_inc(zT_done, 1)

            def make_z(g):
                pe.wait_ge(zT_kept, g)
                for m in range(2):
                    last = nc.tensor.transpose(z_ps[:, P * m:P * m + P], zT_sb[:, P * m:P * m + P], ident[:])
                last.then_inc(z_done, 1)

            def make_logits(g):
                pe.wait_ge(blocks_ready, g)
                pe.wait_ge(z_kept, g)
                columns = z_sb[:].rearrange("p m e -> p (m e)")
                for k in range(GT):
                    m = 2 * (k % 2) + k // 2
                    last = nc.tensor.matmul(logit_ps[:, P * k:P * k + LN], at_blocks[:, k, :],
                                            columns[:, NE * m:NE * m + LN], start=True, stop=True)
                last.then_inc(logits_done, 1)

            def make_out(g, parity, u, n):
                q, k, h = g - 2, u // HH, u % HH
                if u == 0:
                    pe.wait_ge(mixT_ready, q + 1)
                if h == 0:
                    pe.wait_ge(xe_ready, GT * q + k + 1)
                to, back = out_bank(g, u, n)
                if n is not None or UNITS * q + u >= back:
                    pe.wait_ge(out_kept, UNITS * q + u - back + 1)
                for p in range(PAIR):
                    last = nc.tensor.matmul(to[C * p:C * p + C, :], mixT_sb[:, parity, k, C * p:C * p + C],
                                            xe_sb[:, k, p, BANK * h:BANK * h + BANK], start=True, stop=True)
                last.then_inc(out_done, 1)

            def body(g, parity, n=None):
                transposing, routing, putting_out = stages(g, n)
                x_loads = loads(g, parity, n)
                ahead = AHEAD if n is None and g == 2 else 0
                for u in range(UNITS + 1):
                    if transposing and ahead <= u < UNITS:
                        transpose_x(g, parity, u, x_loads, n)
                    if routing and u == 1:
                        make_z(g)
                    if routing and u == (2 if transposing else 1):
                        make_logits(g)
                    if putting_out and u >= 1:
                        make_out(g, parity, u - 1, n)
                if transposing:
                    make_zT(g)

            pe.wait_ge(consts_set, 2)
            pe.wait_ge(net_loaded[0], 48)
            nc.tensor.transpose(condT_ps, cond_sb[:], ident[:]).then_inc(net_pe, 1)
            pe.wait_ge(net_act, 1)
            nc.tensor.matmul(h1_ps, w0_sb[:], condT_sb[:], start=True, stop=True).then_inc(net_pe, 1)
            pe.wait_ge(net_loaded[1], 32)
            pe.wait_ge(net_act, 2)
            nc.tensor.matmul(h2_ps, w1_sb[:], h1T_sb[:], start=True, stop=True).then_inc(net_pe, 1)
            pe.wait_ge(net_loaded[2], 32)
            pe.wait_ge(net_act, 3)
            nc.tensor.matmul(att_ps, h2T_sb[:], w2_sb[:], start=True, stop=True).then_inc(net_pe, 1)
            for u in range(0, HH):
                transpose_x(0, 0, u, 1)
            pe.wait_ge(net_dve, 6)
            nc.tensor.transpose(attT_ps, att_wide[:].rearrange("b p k s -> b (p k s)"), ident[:]).then_inc(net_pe, 1)
            pe.wait_ge(router_loaded, 32)
            for c in range(HC):
                last = nc.tensor.transpose(rT_ps[:, NE * c:NE * c + NE], router_sb[:, P * c:P * c + P], ident[0:NE, 0:NE])
            last.then_inc(rT_done, 1)
            for u in range(HH, 2 * HH):
                transpose_x(0, 0, u, 1)
            pe.wait_ge(net_dve, 8)
            pe.wait_ge(mats_loaded, 16 * 2 * PAIR)
            nc.tensor.matmul(ab_ps, bias_rows[:].rearrange("p a o -> p (a o)"), att_diag[:, 0, :], start=True, stop=True).then_inc(ab_done, 1)
            for s in range(GS):
                if s >= 2:
                    pe.wait_ge((aT_kept_act, aT_kept_dve)[s % 2], s // 2)
                nc.tensor.matmul(out_ps[s % 2][:], w_rows[:, s, :, :].rearrange("p a i -> p (a i)"),
                                 att_diag[:].rearrange("p a j -> p (a j)"), start=True, stop=True).then_inc(aT_done, 1)
                if s + 2 * HH < UNITS:
                    transpose_x(0, 0, s + 2 * HH, 1)
            pe.wait_ge(rT_kept, 1)
            pe.wait_ge(consts_set, 3)
            nc.tensor.matmul(r_sum_ps, ones[:], rT_sb[:].rearrange("p c e -> p (c e)"), start=True, stop=True).then_inc(r_sum_done, 1)
            make_zT(0)
            pe.wait_ge(r_sum_kept, 1)
            pe.wait_ge(aT_kept_act, GS // 2)
            pe.wait_ge(aT_kept_dve, GS // 2)
            pe.wait_ge(zeros_set, 2)
            for u in range(UNITS):
                transpose_x(1, 1, u, 1)
                if u == 1:
                    make_z(1)
                if u == 3:
                    make_logits(1)
            make_zT(1)
            for u in range(AHEAD):
                transpose_x(2, 0, u, 2)
            pe.wait_ge(experts_loaded, 16 * GT * PAIR)
            iterations(pe, body, first=2)


_INS = ['x', 'cond_128', 'L0_cond_W0', 'L0_cond_b0', 'L0_cond_W1', 'L0_cond_b1', 'L0_cond_W2', 'L0_cond_b2',
        'L0_cond_weight', 'L0_cond_bias_k', 'L0_ffn_router_weight', 'L0_ffn_router_bias', 'L0_ffn_expert_bias']
_OUTS = [((B, C, H), 'float32')]


def kernel(**inputs):
    import numpy as _np
    import concourse.bacc as _bacc
    from concourse import mybir as _mybir
    from concourse.bass_utils import run_bass_kernel_spmd as _run

    nc = _bacc.Bacc("TRN2", target_bir_lowering=False, num_devices=1)
    arrays, args = {}, []
    for name in _INS:
        a = _np.ascontiguousarray(inputs[name])
        arrays[f"in_{name}_dram"] = a
        args.append(nc.dram_tensor(f"in_{name}_dram", a.shape, _mybir.dt.from_np(a.dtype), kind="ExternalInput").ap())
    for i, (shape, dtype) in enumerate(_OUTS):
        dt = _mybir.dt.from_np(_np.dtype(dtype))
        args.append(nc.dram_tensor(f"out_{i}_dram", shape, dt, kind="ExternalOutput").ap())
    adaln_ffn_kernel(nc, *args)
    r = _run(nc, [arrays], core_ids=[0])
    got = tuple(r.results[0][f"out_{i}_dram"] for i in range(len(_OUTS)))
    return got[0]
```
